# Optimizing a Trainium2 kernel written in Bass

```python
import numpy as np
import jax
import jax.numpy as jnp

def _softmax(x, axis=-1):
    return jax.nn.softmax(x, axis=axis)

def _gelu(x):
    return jax.nn.gelu(x, approximate=True)

def _silu(x):
    return jax.nn.silu(x)

def _sigmoid(x):
    return jax.nn.sigmoid(x)

def _layernorm(x, axis=-1, eps=1e-05):
    m = jnp.mean(x, axis=axis, keepdims=True)
    v = jnp.var(x, axis=axis, keepdims=True)
    return (x - m) / jnp.sqrt(v + eps)

def _scatter_add(tgt, idx, src, axis=0):
    return tgt.at[idx].add(src)

def _segment_sum(src, seg, n):
    return jax.ops.segment_sum(src, seg, n)
kernel_name = 'mk_vit_tower_cls_d1_tok_img1024_r4_96278c'

def setup_inputs(seed: int=0):
    np.random.seed(seed)
    _w = jnp.asarray

    def _rec_inputs():
        import jax
        import jax.numpy as jnp
        _rk = jax.random.key(seed)
        x = -0.00016672 + 0.999947 * jax.random.normal(jax.random.fold_in(_rk, 1), (64, 3, 96, 96), jnp.float32)
        cls_tok = 0.02 * jax.random.normal(jax.random.fold_in(_rk, 5), (1, 1, 256), jnp.float32)
        return (x, cls_tok)
    x, cls_tok = _rec_inputs()

    def _L0_tok_setup():
        import jax, jax.numpy as jnp
        import numpy as np
        B, C, H, W = (64, 3, 96, 96)
        P = 16
        HP, WP = (H // P, W // P)
        N = HP * WP
        F = C * P * P
        D = 256
        key = jax.random.key(seed)
        k1, k2, k3, k4, k5 = jax.random.split(key, 5)
        data = jax.random.normal(k1, (B, C, H, W), dtype=jnp.float32)
        lim = 1.0 / np.sqrt(F)
        W_lin = jax.random.uniform(k2, (D, F), minval=-lim, maxval=lim, dtype=jnp.float32)
        b_lin = jax.random.uniform(k3, (D,), minval=-lim, maxval=lim, dtype=jnp.float32)
        class_token = jax.random.normal(k4, (1, 1, D), dtype=jnp.float32)
        position_embeddings = jax.random.normal(k5, (1, N + 1, D), dtype=jnp.float32)
        return {'data': data, 'W_lin': W_lin, 'b_lin': b_lin, 'class_token': class_token, 'position_embeddings': position_embeddings}
    _L0_tok_all = _L0_tok_setup()
    _L0_tok_in = {k: v for k, v in _L0_tok_all.items() if k in ('W_lin', 'b_lin', 'class_token', 'position_embeddings')}
    del _L0_tok_all

    def _L0_attn_setup():
        import jax, jax.numpy as jnp
        import numpy as np
        FOCUS = 3
        EPS = 1e-06

        def _norm_last(t):
            return t / jnp.sum(t, axis=-1, keepdims=True)
        key = jax.random.key(seed)
        ks = jax.random.split(key, 6)
        B, N, C = (4, 1024, 256)
        s = 0.02
        return {'x': jax.random.normal(ks[0], (B, N, C), jnp.float32), 'w_qkv': jax.random.normal(ks[1], (3 * C, C), jnp.float32) * s, 'w_proj': jax.random.normal(ks[2], (C, C), jnp.float32) * s, 'b_proj': jax.random.normal(ks[3], (C,), jnp.float32) * s, 'w_dwc': jax.random.normal(ks[4], (C, 3), jnp.float32) * s, 'b_dwc': jax.random.normal(ks[5], (C,), jnp.float32) * s}
    _L0_attn_all = _L0_attn_setup()
    _L0_attn_in = {k: v for k, v in _L0_attn_all.items() if k in ('w_qkv', 'w_proj', 'b_proj', 'w_dwc', 'b_dwc')}
    del _L0_attn_all

    def _L0_ffn_setup():
        import jax, jax.numpy as jnp
        import numpy as np
        TEMPERATURE = 0.5
        CAPACITY_FACTOR = 1.25
        TOP_K = 1
        key = jax.random.key(seed)
        ks = jax.random.split(key, 5)
        B, S, D, H, E = (4, 512, 256, 512, 8)
        s = 0.02
        return {'x': jax.random.normal(ks[0], (B, S, D), jnp.float32), 'gate_w': jax.random.normal(ks[1], (E, D), jnp.float32) * s, 'gate_b': jnp.zeros((E,), jnp.float32), 'rms_w': jnp.ones((E,), jnp.float32), 'w1': jax.random.normal(ks[2], (E, D, H), jnp.float32) * s, 'b1': jnp.zeros((E, H), jnp.float32), 'w2': jax.random.normal(ks[3], (E, H, D), jnp.float32) * s, 'b2': jnp.zeros((E, D), jnp.float32)}
    _L0_ffn_all = _L0_ffn_setup()
    _L0_ffn_in = {k: v for k, v in _L0_ffn_all.items() if k in ('gate_w', 'gate_b', 'rms_w', 'w1', 'b1', 'w2', 'b2')}
    del _L0_ffn_all
    return {'x': x, 'cls_tok': cls_tok, 'L0_tok_W_lin': _L0_tok_in['W_lin'], 'L0_tok_b_lin': _L0_tok_in['b_lin'], 'L0_tok_class_token': _L0_tok_in['class_token'], 'L0_tok_position_embeddings': _L0_tok_in['position_embeddings'], 'L0_attn_w_qkv': _L0_attn_in['w_qkv'], 'L0_attn_w_proj': _L0_attn_in['w_proj'], 'L0_attn_b_proj': _L0_attn_in['b_proj'], 'L0_attn_w_dwc': _L0_attn_in['w_dwc'], 'L0_attn_b_dwc': _L0_attn_in['b_dwc'], 'L0_ffn_gate_w': _L0_ffn_in['gate_w'], 'L0_ffn_gate_b': _L0_ffn_in['gate_b'], 'L0_ffn_rms_w': _L0_ffn_in['rms_w'], 'L0_ffn_w1': _L0_ffn_in['w1'], 'L0_ffn_b1': _L0_ffn_in['b1'], 'L0_ffn_w2': _L0_ffn_in['w2'], 'L0_ffn_b2': _L0_ffn_in['b2']}

def reference(x, cls_tok, L0_tok_W_lin, L0_tok_b_lin, L0_tok_class_token, L0_tok_position_embeddings, L0_attn_w_qkv, L0_attn_w_proj, L0_attn_b_proj, L0_attn_w_dwc, L0_attn_b_dwc, L0_ffn_gate_w, L0_ffn_gate_b, L0_ffn_rms_w, L0_ffn_w1, L0_ffn_b1, L0_ffn_w2, L0_ffn_b2):
    import jax
    import jax.numpy as jnp

    def _L0_tok_ref(data, W_lin, b_lin, class_token, position_embeddings):
        import jax, jax.numpy as jnp
        import numpy as np
        B, C, H, W = (64, 3, 96, 96)
        P = 16
        HP, WP = (H // P, W // P)
        N = HP * WP
        F = C * P * P
        D = 256
        b = data.shape[0]
        x = data.reshape(b, C, HP, P, WP, P)
        x = x.transpose(0, 2, 4, 1, 3, 5).reshape(b, N, F)
        x = jnp.einsum('bnf,df->bnd', x, W_lin) + b_lin
        cls = jnp.broadcast_to(class_token, (b, 1, D))
        out = jnp.concatenate([cls, x], axis=1) + position_embeddings
        return out

    def _L0_attn_ref(x, w_qkv, w_proj, b_proj, w_dwc, b_dwc):
        import jax, jax.numpy as jnp
        import numpy as np
        FOCUS = 3
        EPS = 1e-06

        def _norm_last(t):
            return t / jnp.sum(t, axis=-1, keepdims=True)
        B, N, C = x.shape
        H = 16
        d = C // H
        qkv = jnp.einsum('bnc,oc->bno', x, w_qkv).reshape(B, N, 3, H, d)
        qkv = jnp.transpose(qkv, (2, 0, 3, 1, 4))
        q, k, v = (qkv[0], qkv[1], qkv[2])
        q = _norm_last(jax.nn.relu(q) + EPS)
        k = _norm_last(jax.nn.relu(k) + EPS)
        q = _norm_last(q ** FOCUS)
        k = _norm_last(k ** FOCUS)
        kv = jnp.einsum('bhnd,bhne->bhde', k, v)
        z = 1.0 / (jnp.einsum('bhnd,bhd->bhn', q, k.sum(axis=2)) + EPS)
        out = jnp.einsum('bhnd,bhde,bhn->bhne', q, kv, z)
        out = jnp.transpose(out, (0, 2, 1, 3)).reshape(B, N, C)
        xp = jnp.pad(out, ((0, 0), (1, 1), (0, 0)))
        conv = xp[:, 0:N, :] * w_dwc[:, 0] + xp[:, 1:N + 1, :] * w_dwc[:, 1] + xp[:, 2:N + 2, :] * w_dwc[:, 2] + b_dwc
        out = out + conv
        return jnp.einsum('bnc,oc->bno', out, w_proj) + b_proj

    def _L0_ffn_ref(x, gate_w, gate_b, rms_w, w1, b1, w2, b2):
        import jax, jax.numpy as jnp
        import numpy as np
        TEMPERATURE = 0.5
        CAPACITY_FACTOR = 1.25
        TOP_K = 1
        B, S, D = x.shape
        E = gate_w.shape[0]
        xf = x.reshape(-1, D)
        N = xf.shape[0]
        logits = xf @ gate_w.T + gate_b
        eps = jnp.finfo(logits.dtype).eps
        ms = jnp.mean(logits * logits, axis=-1, keepdims=True)
        logits = logits * jax.lax.rsqrt(ms + eps) * rms_w
        gates = jax.nn.softmax(logits / TEMPERATURE, axis=-1)
        g, idx = jax.lax.top_k(gates, TOP_K)
        g, idx = (g[:, 0], idx[:, 0])
        capacity = min(int(np.ceil(N * TOP_K / E * CAPACITY_FACTOR)), N)
        counts = jnp.zeros((E,), jnp.int32).at[idx].add(1)
        active = (counts > 0) & (capacity >= 1)
        mask = active[idx].astype(gates.dtype)
        masked = g * mask
        norm_g = masked / (masked + 1e-06)
        h = jax.nn.gelu(jnp.einsum('nd,edh->neh', xf, w1) + b1, approximate=False)
        y = jnp.einsum('neh,ehd->ned', h, w2) + b2
        out = (y * norm_g[:, None, None]).sum(axis=1)
        return out.reshape(B, S, D)
    h = _L0_tok_ref(x, L0_tok_W_lin, L0_tok_b_lin, L0_tok_class_token, L0_tok_position_embeddings)
    h = jnp.concatenate([jnp.broadcast_to(cls_tok, (h.shape[0], 1, h.shape[2])), h], axis=1)
    h = h + _L0_attn_ref(_layernorm(h, axis=-1), L0_attn_w_qkv, L0_attn_w_proj, L0_attn_b_proj, L0_attn_w_dwc, L0_attn_b_dwc)
    h = h + _L0_ffn_ref(_layernorm(h, axis=-1), L0_ffn_gate_w, L0_ffn_gate_b, L0_ffn_rms_w, L0_ffn_w1, L0_ffn_b1, L0_ffn_w2, L0_ffn_b2)
    return h

_drawn_inputs = setup_inputs


def setup_inputs(seed=0):
    import zlib

    import numpy as np

    out = dict(_drawn_inputs(seed))
    spreads = {'L0_ffn_gate_b': (0.0, 2.0),
     'L0_ffn_rms_w': (1.0, 0.6),
     'L0_ffn_b1': (0.0, 0.1),
     'L0_ffn_b2': (0.0, 0.1)}
    factors = {'L0_tok_b_lin': 3.157,
     'L0_attn_b_proj': 2.768,
     'L0_attn_w_dwc': 57.012,
     'L0_attn_b_dwc': 6.87,
     'L0_ffn_gate_w': 64.0,
     'cls_tok': 3.844}
    for name, (base, spread) in spreads.items():
        noise = np.random.default_rng([zlib.crc32(name.encode()), seed]).standard_normal(out[name].shape)
        drawn = base * np.exp(spread * noise) if base else spread * noise
        out[name] = jnp.asarray(drawn.astype(out[name].dtype))
    for name, factor in factors.items():
        out[name] = (out[name] * factor).astype(out[name].dtype)
    return out
```

```python
from contextlib import ExitStack

import concourse.bass as bass
from concourse import mybir

F32 = mybir.dt.float32
F32R = mybir.dt.float32r
ALU = mybir.AluOpType
ACT = mybir.ActivationFunctionType
AX = mybir.AxisListType.X

IMAGES, CHAN, SIDE, PATCH = 64, 3, 96, 16
GRID = SIDE // PATCH
PATCHES = GRID * GRID
SEQ = PATCHES + 2
D = 256
KT = D // 128
PIX = CHAN * PATCH * PATCH
PKT = PIX // 128
HEADS, HD = 16, 16
EXPERTS, HID = 8, 512
MT = EXPERTS * HID // 128

CHUNKS = 8
IMG = IMAGES // CHUNKS
TOK = IMG * SEQ
PTOK = IMG * PATCHES
TI = 3
TT = TI * SEQ
TILE0 = [0, 3, 5]
NT = len(TILE0)
HPK = 128 // HD
KVW = TI * 128 + TI
KVE = 2 * NT * KT
NUMW = 128 + HPK

ATT_EPS = 1e-6
LN_EPS = 1e-5
RMS_EPS = 1.1920928955078125e-07
GATE_SCALE = 2.0
NORM_EPS = 1e-6

GBUF = 2
SBUF_G = 3
LAG = 2
STAGES = 4


def kv_bank(j):
    return j if j < 4 else j - 2


def spread(q, t):
    ap = q[:, :, t, :]
    (pitch, parts), (k_step, k_n), _ = ap.ap
    return bass.AP(ap.tensor, ap.offset, [[pitch, parts], [k_step, k_n], [TT + SEQ, TI], [1, SEQ]])


def vit_block(nc, x_p, w_lin, w_qkv, w_proj, gate_w, w_ffn, vecs, b1, rows, consts, out):
    with ExitStack() as ctx:
        def sb(name, shape, dt=F32):
            return ctx.enter_context(nc.sbuf_tensor(name, shape, dt))

        def sem(name):
            return ctx.enter_context(nc.semaphore(name))

        ffn_hi = sb("ffn_hi", [128, MT, 512], F32R)
        ffn_lo = sb("ffn_lo", [128, MT, 512], F32R)
        lin_sb = sb("lin_sb", [128, PKT, D])
        qkv_sb = sb("qkv_sb", [128, KT, 3 * D])
        proj_sb = sb("proj_sb", [128, KT, D])
        gate_sb = sb("gate_sb", [128, KT, 128])
        NV = SEQ - 1 + 1 + 1 + 1 + 3 + 1 + EXPERTS
        vec_sb = sb("vec_sb", [128, KT, NV])
        b1_sb = sb("b1_sb", [128, MT])
        row_sb = sb("row_sb", [TT, D + 2 * EXPERTS])
        con_sb = sb("con_sb", [128, 128 + 128 + HPK + TI])
        ident = con_sb[:, 0:128]
        block_mask = con_sb[:, 128:256]
        head_mask = con_sb[:, 256:256 + HPK]
        img_mask = con_sb[0:TT, 256 + HPK:256 + HPK + TI]
        pos_raw = vec_sb[:, :, 0:SEQ - 1]
        o = SEQ - 1
        class_raw = vec_sb[:, :, o:o + 1]
        cls_raw = vec_sb[:, :, o + 1:o + 2]
        blin_raw = vec_sb[:, :, o + 2:o + 3]
        dwc = vec_sb[:, :, o + 3:o + 6]
        b_dwc = vec_sb[:, :, o + 6:o + 7]
        b2_raw = vec_sb[:, :, o + 7:o + 7 + EXPERTS]
        b_proj = row_sb[:, 0:D]
        gate_b = row_sb[:, D:D + EXPERTS]
        rms_w = row_sb[:, D + EXPERTS:D + 2 * EXPERTS]
        pos_sb = sb("pos_sb", [128, KT, PATCHES])
        w_mid = sb("w_mid", [128, KT])
        b2_sum = sb("b2_sum", [128, KT])
        neg_half = sb("neg_half", [TT, NT])

        feat_h = sb("feat_h", [128, KT, IMG, SEQ])
        tok_hb = sb("tok_hb", [TT, NT, D])
        tok_a = sb("tok_a", [TT, NT, D])
        tok_b = sb("tok_b", [TT, NT, D])
        feat_1 = sb("feat_1", [128, KT, TOK])
        feat_2 = sb("feat_2", [128, KT, TOK])
        feat_3 = sb("feat_3", [128, KT, TOK])
        x2_hi = sb("x2_hi", [128, KT, TOK], F32R)
        x2_lo = sb("x2_lo", [128, KT, TOK], F32R)
        g_hi = sb("g_hi", [128, SBUF_G, TOK], F32R)
        g_lo = sb("g_lo", [128, SBUF_G, TOK], F32R)
        q_spread = sb("q_spread", [128, KT, NT, TI * TT])
        v_masked = sb("v_masked", [TT, 2, KT, KVW])
        kvx = sb("kvx", [128, PKT * PTOK])
        kv_sb = kvx[:, 0:2 * KT * TI * NUMW].rearrange("p (b k i n) -> p b k i n", b=2, k=KT, i=TI)
        x_sb = kvx[:, :].rearrange("p (k n) -> p k n", k=PKT)
        wide = sb("wide", [128, 2 * NT * D + GBUF * TOK])
        tok_h2c = wide[0:TT, 0:NT * D].rearrange("p (t d) -> p t d", t=NT)
        tok_h2n = wide[0:TT, NT * D:2 * NT * D].rearrange("p (t d) -> p t d", t=NT)
        gel = wide[:, 2 * NT * D:].rearrange("p (b n) -> p b n", b=GBUF)
        stage = wide[:, 0:STAGES * 512].rearrange("p (s n) -> p s n", s=STAGES)
        stats = sb("stats", [TT, NT, 6])
        mean = sb("mean", [TT, NT])
        ls = sb("ls", [TT, 5, NT])
        var_e = sb("var_e", [TT, NT])
        rstd = sb("rstd", [TT, NT])
        k_sum = sb("k_sum", [TT, NT * HEADS])
        k_inv = sb("k_inv", [TT, NT * HEADS])
        z_inv = sb("z_inv", [TT, NT * HEADS])
        lg = sb("lg", [TT, 5, NT, EXPERTS])
        gs = sb("gs", [TT, 8, NT])
        gate_n = sb("gate_n", [TT, NT])
        gate_c = sb("gate_c", [TT, NT])

        ps_a = ctx.enter_context(nc.psum_tensor("ps_a", [128, 4, 512], F32))
        ps_h = ctx.enter_context(nc.psum_tensor("ps_h", [128, 2, 512], F32))
        ps_y = ctx.enter_context(nc.psum_tensor("ps_y", [128, KT, 512], F32))
        ps_tok01 = ps_a[0:TT, 0:2, :].rearrange("p b n -> p (b n)")[:, 0:NT * D].rearrange("p (t d) -> p t d", t=NT)
        ps_tok23 = ps_a[0:TT, 2:4, :].rearrange("p b n -> p (b n)")[:, 0:NT * D].rearrange("p (t d) -> p t d", t=NT)
        ps_feat01 = ps_a[:, 0:2, 0:TOK]
        ps_feat23 = ps_a[:, 2:4, 0:TOK]

        ld_small = sem("ld_small")
        ld_lin = sem("ld_lin")
        ld_x = sem("ld_x")
        ld_att = sem("ld_att")
        ld_stage = [sem(f"ld_stage{s}") for s in range(STAGES)]
        w_hi_done = sem("w_hi_done")
        w_lo_done = sem("w_lo_done")
        table = sem("table")
        zeroed_p = sem("zeroed_p")
        zeroed = sem("zeroed")
        patch_ps = sem("patch_ps")
        h_feat = sem("h_feat")
        h_tok = sem("h_tok")
        stat1 = sem("stat1")
        rstd1 = sem("rstd1")
        hb_ready = sem("hb_ready")
        xn1 = sem("xn1")
        x1_ps = sem("x1_ps")
        x1_sb = sem("x1_sb")
        q_ps = sem("q_ps")
        q_relu = sem("q_relu")
        q_sq = sem("q_sq")
        q_cube = sem("q_cube")
        kv_ps = sem("kv_ps")
        k_relu = sem("k_relu")
        k_sq = sem("k_sq")
        k_cube = sem("k_cube")
        k_total = sem("k_total")
        k_recip = sem("k_recip")
        k_norm = sem("k_norm")
        v_ready = sem("v_ready")
        kvp_ps = sem("kvp_ps")
        kvp_sb = sem("kvp_sb")
        num_ps = sem("num_ps")
        z_ready = sem("z_ready")
        o_tok = sem("o_tok")
        o_ps = sem("o_ps")
        c_mid = sem("c_mid")
        c_add = sem("c_add")
        proj_ps = sem("proj_ps")
        h2_ready = sem("h2_ready")
        stat2 = sem("stat2")
        rstd2 = sem("rstd2")
        xn2 = sem("xn2")
        x2_ps = sem("x2_ps")
        x2_f = sem("x2_f")
        logit_ps = sem("logit_ps")
        gate_v = sem("gate_v")
        gate_rms = sem("gate_rms")
        gate_t = sem("gate_t")
        x2_hi_ok = sem("x2_hi_ok")
        x2_lo_ok = sem("x2_lo_ok")
        h2_moved = sem("h2_moved")
        hid_ps = sem("hid_ps")
        gelu_ok = sem("gelu_ok")
        g_hi_ok = sem("g_hi_ok")
        g_lo_ok = sem("g_lo_ok")
        y_part = sem("y_part")
        y_feat = sem("y_feat")
        y_tok = sem("y_tok")
        out_sb = sem("out_sb")
        stored = sem("stored")
        GSTEPS = 15
        LSTEPS = NT + 7
        TABLES = KT + KT + 4 + 2 * KT
        SPLIT = 2

        feat_toks = [slice(SEQ * i, SEQ * i + TT) for i in TILE0]

        block = ctx.enter_context(nc.Block())

        @block.sync
        def _(sp):
            sp.dma_start(x_sb, x_p[0]).then_inc(ld_x, 16)
            sp.dma_start(lin_sb[:, :, :], w_lin).then_inc(ld_lin, 16)
            sp.dma_start(vec_sb[:, :, :], vecs).then_inc(ld_small, 16)
            sp.dma_start(con_sb[:, :], consts).then_inc(ld_small, 16)
            sp.dma_start(row_sb[:, :], rows).then_inc(ld_small, 16)
            sp.dma_start(b1_sb[:, :], b1).then_inc(ld_small, 16)
            sp.dma_start(qkv_sb[:, :, :], w_qkv).then_inc(ld_att, 16)
            sp.dma_start(proj_sb[:, :, :], w_proj).then_inc(ld_att, 16)
            sp.dma_start(gate_sb[:, :, :], gate_w).then_inc(ld_att, 16)
            for m in range(MT):
                if m >= STAGES:
                    sp.wait_ge(w_lo_done, m - STAGES + 1)
                sp.dma_start(stage[:, m % STAGES, :], w_ffn[m]).then_inc(ld_stage[m % STAGES], 16)
            sp.wait_ge(num_ps, NT)
            sp.dma_start(x_sb, x_p[1]).then_inc(ld_x, 16)

            def load_next(c):
                sp.wait_ge(num_ps, (c + 1) * NT + NT)
                sp.dma_start(x_sb, x_p[c + 2]).then_inc(ld_x, 16)

            def store(c):
                sp.wait_ge(out_sb, c * NT + NT)
                sp.dma_start(out[c, 0:2 * TT, :].rearrange("(t p) d -> p t d", t=2),
                             tok_b[:, 0:2, :]).then_inc(stored, 16)
                sp.dma_start(out[c, 2 * TT:TOK, :], tok_b[3 * TT - TOK:TT, 2, :]).then_inc(stored, 16)

            with sp.Fori(0, CHUNKS - 2) as c:
                load_next(c)
                store(c)
            store(CHUNKS - 2)
            store(CHUNKS - 1)
            sp.wait_ge(stored, 32 * CHUNKS + 32)

        @block.tensor
        def _(pe):
            def patch(p, mt):
                if mt == 0:
                    pe.wait_ge(ld_x, 16 * p + 16)
                for k in range(PKT):
                    mm = pe.matmul(ps_a[:, mt, 0:PTOK], lin_sb[:, k, mt * 128:mt * 128 + 128],
                                   x_sb[:, k, :], start=(k == 0), stop=(k == PKT - 1))
                mm.then_inc(patch_ps, 1)

            def to_tok(dst, src, done):
                for t in range(NT):
                    for k in range(KT):
                        mm = pe.transpose(dst[:, t, k * 128:k * 128 + 128], src[:, k, feat_toks[t]], ident)
                mm.then_inc(done, 1)

            def to_feat(dst, src, done):
                for t in range(NT):
                    for k in range(KT):
                        mm = pe.transpose(dst[:, k, feat_toks[t]], src[:, t, k * 128:k * 128 + 128],
                                          ident[0:TT, 0:TT])
                mm.then_inc(done, 1)

            def kv_tiles(tiles):
                for t in tiles:
                    for k in range(KT):
                        mm = pe.matmul(ps_a[0:TT, 1 + t, :], feat_1[:, k, feat_toks[t]],
                                       qkv_sb[:, k, D:3 * D], start=(k == 0), stop=(k == KT - 1))
                    mm.then_inc(kv_ps, 1)

            def kv_product(a, j):
                t, k = j // KT, j % KT
                if k == 0 or j == 3:
                    pe.wait_ge(v_ready, a * NT + (NT if j >= 3 else t + 1))
                if j >= 4:
                    pe.wait_ge(kvp_sb, a * KVE + 2 * (j - 2) + 2)
                pe.matmul(ps_a[:, kv_bank(j), 0:KVW], tok_a[:, t, k * 128:k * 128 + 128],
                          v_masked[:, t % 2, k, :], start=True, stop=True).then_inc(kvp_ps, 1)

            def attend(a, s):
                if s == 0:
                    pe.wait_ge(h_feat, a * KT + KT)
                    to_tok(ps_tok01, feat_h[:, :, :, :].rearrange("p k i s -> p k (i s)"), h_tok)
                if s == 3:
                    pe.wait_ge(xn1, a * NT + NT)
                    to_feat(ps_feat23, tok_a, x1_ps)
                if s == 5:
                    pe.wait_ge(x1_sb, a + 1)
                    pe.wait_ge(hb_ready, a + 1)
                    for mt in range(KT):
                        for k in range(KT):
                            mm = pe.matmul(ps_a[:, mt, 0:TOK], qkv_sb[:, k, mt * 128:mt * 128 + 128],
                                           feat_1[:, k, :], start=(k == 0), stop=(k == KT - 1))
                    mm.then_inc(q_ps, 1)
                if s == 7:
                    pe.wait_ge(q_relu, a + 1)
                    kv_tiles([0, 1])
                if s == 8:
                    kv_tiles([2])
                if s == 12:
                    pe.wait_ge(k_norm, a + 1)
                    kv_product(a, 0)
                    kv_product(a, 1)
                    kv_product(a, 2)
                if s == 14:
                    kv_product(a, 3)
                if s == 15:
                    kv_product(a, 4)
                if s == 16:
                    kv_product(a, 5)
                if s in (16, 17, 18):
                    t = s - 16
                    pe.wait_ge(q_cube, a * NT + t + 1)
                    pe.wait_ge(kvp_sb, a * KVE + 2 * KT * (t + 1))
                    for k in range(KT):
                        for i in range(TI):
                            mm = pe.matmul(ps_a[0:TT, t, k * 256:k * 256 + NUMW],
                                           q_spread[:, k, t, i * TT:i * TT + TT],
                                           kv_sb[:, t % 2, k, i, :], start=(i == 0), stop=(i == TI - 1))
                    mm.then_inc(num_ps, 1)
                if s == 20:
                    pe.wait_ge(o_tok, a + 1)
                    to_feat(ps_feat23, tok_a, o_ps)
                if s == 23:
                    pe.wait_ge(c_add, a * 2 * KT + 2 * KT)
                    for t in range(NT):
                        for k in range(KT):
                            mm = pe.matmul(ps_tok01[:, t, :], feat_1[:, k, feat_toks[t]], proj_sb[:, k, :],
                                           start=(k == 0), stop=(k == KT - 1))
                    mm.then_inc(proj_ps, 1)
                if s == 26:
                    pe.wait_ge(xn2, a * NT + NT)
                    to_feat(ps_feat23, tok_a, x2_ps)
                if s == 28:
                    pe.wait_ge(x2_f, a + 1)
                    for t in range(NT):
                        for k in range(KT):
                            mm = pe.matmul(ps_a[0:TT, 0, t * 128:t * 128 + 128], feat_2[:, k, feat_toks[t]],
                                           gate_sb[:, k, :], start=(k == 0), stop=(k == KT - 1))
                    mm.then_inc(logit_ps, 1)

            def three_passes(dst, w_cols, m, hi, lo, first, last):
                for n, (w, x) in enumerate(((ffn_hi, hi), (ffn_lo, hi), (ffn_hi, lo))):
                    mm = pe.matmul(dst, w[:, m, w_cols], x, start=(first and n == 0), stop=(last and n == 2))
                return mm

            def hidden(c, m):
                if m == 0:
                    pe.wait_ge(x2_lo_ok, c + 1)
                if m >= 2:
                    pe.wait_ge(gelu_ok, c * MT + m - 1)
                for k in range(KT):
                    mm = three_passes(ps_h[:, m % 2, 0:TOK], slice(k * 128, k * 128 + 128), m,
                                      x2_hi[:, k, :], x2_lo[:, k, :], k == 0, k == KT - 1)
                mm.then_inc(hid_ps, 1)

            def back(c, m):
                pe.wait_ge(g_lo_ok, c * MT + m + 1)
                for k in range(KT):
                    mm = three_passes(ps_y[:, k, 0:TOK], slice(256 + k * 128, 256 + k * 128 + 128), m,
                                      g_hi[:, m % SBUF_G, :], g_lo[:, m % SBUF_G, :], m == 0, m == MT - 1)
                mm.then_inc(y_part, 1)

            def body(c, with_attend, with_patch):
                for m in range(MT):
                    hidden(c, m)
                    if with_attend:
                        attend(c + 1, m)
                    if m >= LAG:
                        back(c, m - LAG)
                if with_patch:
                    pe.wait_ge(gate_v, (c + 1) * GSTEPS + 1)
                    patch(c + 2, 0)
                for m in range(MT - LAG, MT):
                    back(c, m)
                if with_patch:
                    patch(c + 2, 1)
                pe.wait_ge(y_feat, c * KT + KT)
                to_tok(ps_tok23, feat_1, y_tok)

            pe.wait_ge(ld_lin, 16)
            for mt in range(KT):
                patch(0, mt)
            pe.wait_ge(ld_att, 48)
            pe.wait_ge(table, TABLES)
            pe.wait_ge(zeroed, 1)
            pe.wait_ge(ld_small, 64)
            for s in range(MT):
                attend(0, s)
            pe.wait_ge(gate_v, 1)
            for mt in range(KT):
                patch(1, mt)
            pe.wait_ge(w_lo_done, MT)
            with pe.Fori(0, CHUNKS - 2) as c:
                body(c, True, True)
            body(CHUNKS - 2, True, False)
            body(CHUNKS - 1, False, False)

        @block.scalar
        def _(act):
            def attend(a, s, c=None):
                if s == 4:
                    act.wait_ge(x1_ps, a + 1)
                    act.activation(feat_1[:, :, :], ps_feat23, ACT.Copy).then_inc(x1_sb, 1)
                if s == 6:
                    act.wait_ge(q_relu, a + 1)
                    act.activation(feat_3[:, :, :], feat_2[:, :, :], ACT.Square).then_inc(q_sq, 1)
                if s in (9, 10, 13):
                    t = {9: 0, 10: 1, 13: 2}[s]
                    if t == 0:
                        act.wait_ge(k_relu, a + 1)
                        if c is not None:
                            act.wait_ge(stored, 32 * c + 32)
                        act.activation(tok_b[:, :, :], tok_a[:, :, :], ACT.Square).then_inc(k_sq, 1)
                    if t == 2:
                        act.wait_ge(kvp_ps, a * NT * KT + KT)
                    for i in range(TI):
                        v = act.activation(v_masked[:, t % 2, :, i * 128:i * 128 + 128],
                                           ps_a[0:TT, 1 + t, D:2 * D].rearrange("p (k e) -> p k e", k=KT),
                                           ACT.Copy, scale=img_mask[:, i:i + 1])
                    v.then_inc(v_ready, 1)
                if s == 21:
                    act.wait_ge(o_ps, a + 1)
                    for k in range(KT):
                        act.activation(feat_1[:, k, :], ps_a[:, 2 + k, 0:TOK], ACT.Identity,
                                       bias=b_dwc[:, k, :], scale=w_mid[:, k:k + 1]).then_inc(c_mid, 1)
                if s == 27:
                    act.wait_ge(x2_ps, a + 1)
                    act.activation(feat_2[:, :, :], ps_feat23, ACT.Copy).then_inc(x2_f, 1)
                if s == 31:
                    act.wait_ge(gate_v, a * GSTEPS + 8)
                    act.activation(lg[:, 2, :, :], lg[:, 1, :, :], ACT.Tanh, scale=GATE_SCALE / 2).then_inc(gate_t, 1)

            def take_over(a):
                act.wait_ge(h2_ready, a + 1)
                act.activation(tok_h2c, tok_h2n, ACT.Copy).then_inc(h2_moved, 1)
                act.wait_ge(gate_v, a * GSTEPS + GSTEPS)
                act.activation(gate_c[:, :], gate_n[:, :], ACT.Copy).then_inc(h2_moved, 1)

            def body(c, with_attend):
                for m in range(MT):
                    act.wait_ge(hid_ps, c * MT + m + 1)
                    if m >= GBUF:
                        act.wait_ge(g_lo_ok, c * MT + m - GBUF + 1)
                    act.activation(gel[:, m % GBUF, :], ps_h[:, m % 2, 0:TOK], ACT.Gelu,
                                   bias=b1_sb[:, m:m + 1]).then_inc(gelu_ok, 1)
                    if with_attend:
                        attend(c + 1, m, c)
                act.wait_ge(y_part, c * MT + MT)
                for k in range(KT):
                    act.activation(feat_1[:, k, :], ps_y[:, k, 0:TOK], ACT.Identity,
                                   bias=b2_sum[:, k:k + 1]).then_inc(y_feat, 1)
                if with_attend:
                    act.wait_ge(out_sb, c * NT + NT)
                    take_over(c + 1)

            act.wait_ge(ld_small, 64)
            act.wait_ge(table, TABLES)
            for s in range(MT):
                for m in range(SPLIT * s, min(SPLIT * s + SPLIT, MT)):
                    act.wait_ge(ld_stage[m % STAGES], 16 * (m // STAGES) + 16)
                    act.activation(ffn_hi[:, m, :], stage[:, m % STAGES, :], ACT.Copy).then_inc(w_hi_done, 1)
                attend(0, s)
            take_over(0)
            with act.Fori(0, CHUNKS - 2) as c:
                body(c, True)
            body(CHUNKS - 2, True)
            body(CHUNKS - 1, False)

        @block.vector
        def _(dve):
            def f32(ap):
                return ap.bitcast(F32)

            def layer_stats(a, src, stat):
                base = a * LSTEPS
                for t in range(NT):
                    dve.bn_stats(stats[:, t, :], src[:, t, :]).then_inc(stat, 1)
                dve.wait_ge(stat, base + NT)
                dve.tensor_tensor(ls[:, 0, :], stats[:, :, 1], stats[:, :, 4], ALU.add).then_inc(stat, 1)
                dve.tensor_tensor(ls[:, 1, :], stats[:, :, 1], stats[:, :, 4], ALU.subtract).then_inc(stat, 1)
                dve.tensor_tensor(ls[:, 2, :], stats[:, :, 2], stats[:, :, 5], ALU.add).then_inc(stat, 1)
                dve.wait_ge(stat, base + NT + 3)
                dve.tensor_tensor(ls[:, 3, :], ls[:, 1, :], ls[:, 1, :], ALU.mult).then_inc(stat, 1)
                dve.tensor_scalar(ls[:, 4, :], ls[:, 2, :], 1.0 / D, LN_EPS, ALU.mult, ALU.add).then_inc(stat, 1)
                dve.tensor_scalar(mean[:, :], ls[:, 0, :], 0.5, None, ALU.mult).then_inc(stat, 1)
                dve.wait_ge(stat, base + NT + 6)
                dve.scalar_tensor_tensor(out=var_e[:, :], in0=ls[:, 3, :], scalar=0.25, in1=ls[:, 4, :],
                                         op0=ALU.mult, op1=ALU.add).then_inc(stat, 1)

            def normalise(a, src, done):
                for t in range(NT):
                    dve.tensor_scalar(tok_a[:, t, :], src[:, t, :], mean[:, t:t + 1], rstd[:, t:t + 1],
                                      ALU.subtract, ALU.mult).then_inc(done, 1)

            def kv_evacuate(a, j):
                t, k = j // KT, j % KT
                dve.wait_ge(kvp_ps, a * NT * KT + j + 1)
                if j == 2 * KT:
                    dve.wait_ge(num_ps, a * NT + 1)
                ps = ps_a[:, kv_bank(j), 0:KVW]
                dve.tensor_tensor(kv_sb[:, t % 2, k, :, 0:128],
                                  ps[:, 0:TI * 128].rearrange("p (i e) -> p i e", i=TI),
                                  block_mask.unsqueeze(1).to_broadcast([128, TI, 128]), ALU.mult).then_inc(kvp_sb, 1)
                dve.scalar_tensor_tensor(out=kv_sb[:, t % 2, k, :, 128:NUMW],
                                         in0=ps[:, TI * 128:TI * 128 + TI].unsqueeze(2).to_broadcast([128, TI, HPK]),
                                         scalar=ATT_EPS,
                                         in1=head_mask.unsqueeze(1).to_broadcast([128, TI, HPK]),
                                         op0=ALU.add, op1=ALU.mult).then_inc(kvp_sb, 1)

            def attend(a, s):
                heads = lambda ap: ap.rearrange("p t (h e) -> p (t h) e", e=HD)
                if s == 1:
                    dve.wait_ge(h_tok, a + 1)
                    layer_stats(a, ps_tok01, stat1)
                    dve.tensor_tensor(tok_hb[:, :, :], ps_tok01,
                                      b_proj.unsqueeze(1).to_broadcast([TT, NT, D]), ALU.add).then_inc(hb_ready, 1)
                if s == 2:
                    dve.wait_ge(rstd1, a + 1)
                    normalise(a, ps_tok01, xn1)
                if s == 6:
                    dve.wait_ge(q_ps, a + 1)
                    dve.tensor_scalar(feat_2[:, :, :], ps_feat01, 0.0, ATT_EPS, ALU.max, ALU.add).then_inc(q_relu, 1)
                if s == 7:
                    dve.wait_ge(q_sq, a + 1)
                    for t in range(NT):
                        dve.tensor_tensor(spread(q_spread, t),
                                          feat_3[:, :, feat_toks[t]].rearrange("p k (i s) -> p k i s", i=TI),
                                          feat_2[:, :, feat_toks[t]].rearrange("p k (i s) -> p k i s", i=TI),
                                          ALU.mult).then_inc(q_cube, 1)
                if s == 9:
                    dve.wait_ge(kv_ps, a * NT + NT)
                    dve.tensor_scalar(tok_a[:, :, :], ps_a[0:TT, 1:4, 0:D], 0.0, ATT_EPS,
                                      ALU.max, ALU.add).then_inc(k_relu, 1)
                if s == 10:
                    dve.wait_ge(k_sq, a + 1)
                    dve.tensor_tensor(tok_b[:, :, :], tok_b[:, :, :], tok_a[:, :, :], ALU.mult).then_inc(k_cube, 1)
                    dve.wait_ge(k_cube, a + 1)
                    dve.tensor_reduce(k_sum[:, :], heads(tok_b[:, :, :]), AX, ALU.add).then_inc(k_total, 1)
                if s == 11:
                    dve.wait_ge(k_total, a + 1)
                    dve.reciprocal(k_inv[:, :], k_sum[:, :]).then_inc(k_recip, 1)
                    dve.wait_ge(k_recip, a + 1)
                    dve.tensor_tensor(heads(tok_a[:, :, :]), heads(tok_b[:, :, :]),
                                      k_inv[:, :].unsqueeze(2).to_broadcast([TT, NT * HEADS, HD]),
                                      ALU.mult).then_inc(k_norm, 1)
                if s == 13:
                    for j in (0, 1, 2):
                        kv_evacuate(a, j)
                if s == 15:
                    kv_evacuate(a, 3)
                if s == 17:
                    for j in (4, 5):
                        kv_evacuate(a, j)
                if s == 19:
                    dve.wait_ge(num_ps, a * NT + NT)
                    halves = ps_a[0:TT, 0:NT, :].rearrange("p t (k n) -> p (t k) n", k=KT)
                    z = z_inv[:, :].rearrange("p (g h) -> p g h", h=HPK)
                    dve.reciprocal(z, halves[:, :, 128:NUMW]).then_inc(z_ready, 1)
                    dve.wait_ge(z_ready, a + 1)
                    dve.tensor_tensor(tok_a[:, :, :].rearrange("p t (k h e) -> p (t k) h e", k=KT, e=HD),
                                      halves[:, :, 0:128].rearrange("p g (h e) -> p g h e", e=HD),
                                      z.unsqueeze(3).to_broadcast([TT, NT * KT, HPK, HD]), ALU.mult).then_inc(o_tok, 1)
                if s == 21:
                    o_img = ps_feat23.rearrange("p k (i s) -> p k i s", s=SEQ)
                    c_img = feat_1[:, :, :].rearrange("p k (i s) -> p k i s", s=SEQ)
                    for side in range(2):
                        for k in range(KT):
                            dst = c_img[:, k, :, 1:SEQ] if side == 0 else c_img[:, k, :, 0:SEQ - 1]
                            src = o_img[:, k, :, 0:SEQ - 1] if side == 0 else o_img[:, k, :, 1:SEQ]
                            if side == 0:
                                dve.wait_ge(c_mid, a * KT + k + 1)
                            else:
                                dve.wait_ge(c_add, a * 2 * KT + k + 1)
                            dve.scalar_tensor_tensor(out=dst, in0=src, scalar=dwc[:, k, 2 * side:2 * side + 1],
                                                     in1=dst, op0=ALU.mult, op1=ALU.add).then_inc(c_add, 1)
                if s == 24:
                    dve.wait_ge(proj_ps, a + 1)
                    dve.wait_ge(h2_moved, 2 * a)
                    dve.wait_ge(hb_ready, a + 1)
                    dve.tensor_tensor(tok_h2n, ps_tok01, tok_hb[:, :, :], ALU.add).then_inc(h2_ready, 1)
                    dve.wait_ge(h2_ready, a + 1)
                    layer_stats(a, tok_h2n, stat2)
                if s == 25:
                    dve.wait_ge(rstd2, a + 1)
                    normalise(a, tok_h2n, xn2)
                if s == 29:
                    dve.wait_ge(logit_ps, a + 1)
                    logits = ps_a[0:TT, 0, 0:NT * 128].rearrange("p (t n) -> p t n", t=NT)[:, :, 0:EXPERTS]
                    dve.tensor_tensor(lg[:, 0, :, :], logits,
                                      gate_b.unsqueeze(1).to_broadcast([TT, NT, EXPERTS]), ALU.add).then_inc(gate_v, 1)
                    dve.wait_ge(gate_v, a * GSTEPS + 1)
                    dve.tensor_tensor(lg[:, 1, :, :], lg[:, 0, :, :], lg[:, 0, :, :], ALU.mult).then_inc(gate_v, 1)
                    dve.wait_ge(gate_v, a * GSTEPS + 2)
                    dve.tensor_reduce(gs[:, 0, :], lg[:, 1, :, :], AX, ALU.add).then_inc(gate_v, 1)
                    dve.wait_ge(gate_v, a * GSTEPS + 3)
                    dve.tensor_scalar(gs[:, 1, :], gs[:, 0, :], 1.0 / EXPERTS, RMS_EPS,
                                      ALU.mult, ALU.add).then_inc(gate_v, 1)
                if s == 30:
                    dve.wait_ge(gate_rms, a + 1)
                    dve.tensor_tensor(lg[:, 3, :, :], lg[:, 0, :, :],
                                      gs[:, 2, :].unsqueeze(2).to_broadcast([TT, NT, EXPERTS]),
                                      ALU.mult).then_inc(gate_v, 1)
                    dve.wait_ge(gate_v, a * GSTEPS + 5)
                    dve.tensor_tensor(lg[:, 4, :, :], lg[:, 3, :, :],
                                      rms_w.unsqueeze(1).to_broadcast([TT, NT, EXPERTS]), ALU.mult).then_inc(gate_v, 1)
                    dve.wait_ge(gate_v, a * GSTEPS + 6)
                    dve.tensor_reduce(gs[:, 3, :], lg[:, 4, :, :], AX, ALU.max).then_inc(gate_v, 1)
                    dve.wait_ge(gate_v, a * GSTEPS + 7)
                    dve.tensor_tensor(lg[:, 1, :, :], lg[:, 4, :, :],
                                      gs[:, 3, :].unsqueeze(2).to_broadcast([TT, NT, EXPERTS]),
                                      ALU.subtract).then_inc(gate_v, 1)

            def gate_end(a):
                dve.wait_ge(gate_t, a + 1)
                dve.tensor_scalar(lg[:, 0, :, :], lg[:, 2, :, :], 1.0, None, ALU.add).then_inc(gate_v, 1)
                dve.tensor_scalar(lg[:, 3, :, :], lg[:, 2, :, :], -1.0, 1.0, ALU.mult, ALU.add).then_inc(gate_v, 1)
                dve.wait_ge(gate_v, a * GSTEPS + 10)
                dve.reciprocal(lg[:, 4, :, :], lg[:, 3, :, :]).then_inc(gate_v, 1)
                dve.wait_ge(gate_v, a * GSTEPS + 11)
                dve.tensor_tensor(lg[:, 1, :, :], lg[:, 0, :, :], lg[:, 4, :, :], ALU.mult).then_inc(gate_v, 1)
                dve.wait_ge(gate_v, a * GSTEPS + 12)
                dve.tensor_reduce(gs[:, 4, :], lg[:, 1, :, :], AX, ALU.add).then_inc(gate_v, 1)
                dve.wait_ge(gate_v, a * GSTEPS + 13)
                dve.tensor_scalar(gs[:, 5, :], gs[:, 4, :], NORM_EPS, 1.0, ALU.mult, ALU.add).then_inc(gate_v, 1)
                dve.wait_ge(gate_v, a * GSTEPS + 14)
                dve.reciprocal(gate_n[:, :], gs[:, 5, :]).then_inc(gate_v, 1)

            def split_input(a, running):
                dve.wait_ge(x2_f, a + 1)
                if running:
                    dve.wait_ge(hid_ps, a * MT)
                dve.tensor_copy(x2_hi[:, :, :], feat_2[:, :, :]).then_inc(x2_hi_ok, 1)
                dve.wait_ge(x2_hi_ok, a + 1)
                dve.tensor_tensor(x2_lo[:, :, :], feat_2[:, :, :], f32(x2_hi[:, :, :]),
                                  ALU.subtract).then_inc(x2_lo_ok, 1)

            def add_position(p):
                for k in range(KT):
                    dve.wait_ge(patch_ps, p * KT + k + 1)
                    dve.tensor_tensor(feat_h[:, k, :, 2:SEQ],
                                      ps_a[:, k, 0:PTOK].rearrange("p (i s) -> p i s", i=IMG),
                                      pos_sb[:, k, :].unsqueeze(1).to_broadcast([128, IMG, PATCHES]),
                                      ALU.add).then_inc(h_feat, 1)

            def body(c, with_attend, with_patch):
                for m in range(MT):
                    dve.wait_ge(gelu_ok, c * MT + m + 1)
                    if m >= SBUF_G:
                        dve.wait_ge(y_part, c * MT + m - SBUF_G + 1)
                    dve.tensor_copy(g_hi[:, m % SBUF_G, :], gel[:, m % GBUF, :]).then_inc(g_hi_ok, 1)
                    dve.wait_ge(g_hi_ok, c * MT + m + 1)
                    dve.tensor_tensor(g_lo[:, m % SBUF_G, :], gel[:, m % GBUF, :], f32(g_hi[:, m % SBUF_G, :]),
                                      ALU.subtract).then_inc(g_lo_ok, 1)
                    if with_attend:
                        attend(c + 1, m)
                if with_attend:
                    split_input(c + 1, True)
                    gate_end(c + 1)
                if with_patch:
                    add_position(c + 2)
                dve.wait_ge(y_tok, c + 1)
                dve.wait_ge(h2_moved, 2 * c + 2)
                dve.wait_ge(stored, 32 * c + 32)
                for t in range(NT):
                    dve.scalar_tensor_tensor(out=tok_b[:, t, :], in0=ps_tok23[:, t, :], scalar=gate_c[:, t:t + 1],
                                             in1=tok_h2c[:, t, :], op0=ALU.mult, op1=ALU.add).then_inc(out_sb, 1)

            dve.wait_ge(ld_small, 64)
            for k in range(KT):
                dve.tensor_scalar(pos_sb[:, k, :], pos_raw[:, k, 1:SEQ - 1], blin_raw[:, k, :], None,
                                  ALU.add).then_inc(table, 1)
            for k in range(KT):
                dve.tensor_scalar(feat_h[:, k, :, 1], class_raw[:, k, :].to_broadcast([128, IMG]),
                                  pos_raw[:, k, 0:1], None, ALU.add).then_inc(table, 1)
            dve.tensor_copy(feat_h[:, 0, :, 0], cls_raw[:, 0, :].to_broadcast([128, IMG])).then_inc(table, 1)
            dve.tensor_copy(feat_h[:, 1, :, 0], cls_raw[:, 1, :].to_broadcast([128, IMG])).then_inc(table, 1)
            dve.tensor_scalar(w_mid[:, :], dwc[:, :, 1], 1.0, None, ALU.add).then_inc(table, 1)
            dve.tensor_reduce(b2_sum[:, :], b2_raw, AX, ALU.add).then_inc(table, 1)
            for b in range(2):
                for k in range(KT):
                    dve.tensor_copy(v_masked[:, b, k, TI * 128:KVW], img_mask).then_inc(table, 1)
            dve.wait_ge(table, TABLES)
            dve.wait_ge(zeroed, 1)
            add_position(0)
            for s in range(MT):
                for m in range(SPLIT * s, min(SPLIT * s + SPLIT, MT)):
                    dve.wait_ge(w_hi_done, m + 1)
                    dve.tensor_tensor(ffn_lo[:, m, :], stage[:, m % STAGES, :], f32(ffn_hi[:, m, :]),
                                      ALU.subtract).then_inc(w_lo_done, 1)
                attend(0, s)
            split_input(0, False)
            gate_end(0)
            add_position(1)
            with dve.Fori(0, CHUNKS - 2) as c:
                body(c, True, True)
            body(CHUNKS - 2, True, False)
            body(CHUNKS - 1, False, False)

        @block.gpsimd
        def _(pool):
            pool.memset(q_spread[:, :, :, :], 0.0).then_inc(zeroed_p, 1)
            pool.memset(neg_half[:, :], -0.5).then_inc(zeroed_p, 1)
            pool.wait_ge(zeroed_p, 2)
            pool.sem_inc(zeroed, 1)
            pool.sem_inc(stored, 32)

            def powers(a):
                pool.wait_ge(stat1, a * LSTEPS + LSTEPS)
                pool.tensor_tensor(rstd[:, :], var_e[:, :], neg_half[:, :], ALU.pow).then_inc(rstd1, 1)
                pool.wait_ge(stat2, a * LSTEPS + LSTEPS)
                pool.tensor_tensor(rstd[:, :], var_e[:, :], neg_half[:, :], ALU.pow).then_inc(rstd2, 1)
                pool.wait_ge(gate_v, a * GSTEPS + 4)
                pool.tensor_tensor(gs[:, 2, :], gs[:, 1, :], neg_half[:, :], ALU.pow).then_inc(gate_rms, 1)

            powers(0)
            with pool.Fori(1, CHUNKS) as a:
                powers(a)


def kernel(**inputs):
    import numpy as np
    import concourse.bacc as bacc
    from concourse.bass_utils import run_bass_kernel_spmd

    g = {n: np.asarray(v) for n, v in inputs.items()}

    def rows_on_partitions(w):
        return w.reshape(-1, 128, w.shape[-1]).transpose(1, 0, 2)

    x = g["x"].reshape(CHUNKS, IMG, CHAN, GRID, PATCH, GRID, PATCH).transpose(0, 2, 4, 6, 1, 3, 5)
    x = x.reshape(CHUNKS, PKT, 128, PTOK).transpose(0, 2, 1, 3)
    gate = np.zeros((D, 128), g["L0_ffn_gate_w"].dtype)
    gate[:, :EXPERTS] = g["L0_ffn_gate_w"].T
    w1 = g["L0_ffn_w1"].transpose(1, 0, 2).reshape(KT, 128, MT, 128).transpose(2, 1, 0, 3).reshape(MT, 128, D)
    w2 = g["L0_ffn_w2"].reshape(MT, 128, D)
    vecs = np.concatenate([g["L0_tok_position_embeddings"][0].T, g["L0_tok_class_token"][0].T, g["cls_tok"][0].T,
                           g["L0_tok_b_lin"][:, None], g["L0_attn_w_dwc"], g["L0_attn_b_dwc"][:, None],
                           g["L0_ffn_b2"].T], axis=1)
    rows = np.concatenate([g["L0_attn_b_proj"], g["L0_ffn_gate_b"], g["L0_ffn_rms_w"]])
    heads = np.arange(128) // HD
    consts = np.concatenate([np.eye(128), heads[:, None] == heads[None, :],
                             heads[:, None] == np.arange(HPK)[None, :],
                             np.arange(128)[:, None] // SEQ == np.arange(TI)[None, :]], axis=1).astype(np.float32)
    sent = {
        "x_p": x,
        "w_lin": rows_on_partitions(g["L0_tok_W_lin"].T),
        "w_qkv": rows_on_partitions(g["L0_attn_w_qkv"].T),
        "w_proj": rows_on_partitions(g["L0_attn_w_proj"].T),
        "gate_w": rows_on_partitions(gate),
        "w_ffn": np.concatenate([w1, w2], axis=2),
        "vecs": rows_on_partitions(vecs),
        "b1": g["L0_ffn_b1"].reshape(MT, 128).T,
        "rows": np.broadcast_to(rows, (TT, rows.size)),
        "consts": consts,
    }
    nc = bacc.Bacc("TRN2", target_bir_lowering=False, num_devices=1)
    sent = {n: np.ascontiguousarray(v) for n, v in sent.items()}
    args = {n: nc.dram_tensor(n, v.shape, mybir.dt.from_np(v.dtype), kind="ExternalInput").ap() for n, v in sent.items()}
    out = nc.dram_tensor("out", (IMAGES, SEQ, D), F32, kind="ExternalOutput").ap()
    vit_block(nc, out=out.rearrange("(c i) s d -> c (i s) d", c=CHUNKS), **args)
    r = run_bass_kernel_spmd(nc, [sent], core_ids=[0])
    return r.results[0]["out"]
```

```python
from contextlib import ExitStack

import concourse.bass as bass
from concourse import mybir

F32 = mybir.dt.float32
F32R = mybir.dt.float32r
ALU = mybir.AluOpType
ACT = mybir.ActivationFunctionType
AX = mybir.AxisListType.X

IMAGES, CHAN, SIDE, PATCH = 64, 3, 96, 16
GRID = SIDE // PATCH
PATCHES = GRID * GRID
SEQ = PATCHES + 2
D = 256
KT = D // 128
PIX = CHAN * PATCH * PATCH
PKT = PIX // 128
HEADS, HD = 16, 16
EXPERTS, HID = 8, 512
MT = EXPERTS * HID // 128
ATT_PIECES = 4
PIECES = ATT_PIECES + MT

CHUNKS = 8
IMG = IMAGES // CHUNKS
TOK = IMG * SEQ
PTOK = IMG * PATCHES
TI = 3
TT = TI * SEQ
TILE0 = [0, 3, 5]
NT = len(TILE0)
HPK = 128 // HD
KVW = TI * 128 + TI
DUP = 128
KVE = 2 * NT * KT
NUMW = 128 + HPK

ATT_EPS = 1e-6
LN_EPS = 1e-5
RMS_EPS = 1.1920928955078125e-07
GATE_SCALE = 2.0
NORM_EPS = 1e-6

GBUF = 2
SBUF_G = 3
LAG = 2
LATE = (4, 9, 20, 23, 28)
STAGES = 4


def kv_bank(j):
    return (1, 0, 2, 1, 0, 3)[j]


def spread(q, t):
    ap = q[:, :, t, :]
    (pitch, parts), (k_step, k_n), _ = ap.ap
    return bass.AP(ap.tensor, ap.offset, [[pitch, parts], [k_step, k_n], [TT + SEQ, TI], [1, SEQ]])


def vit_block(nc, x_p, w_lin, gate_w, w_pieces, vecs, b1, rows, consts, out):
    with ExitStack() as ctx:
        def sb(name, shape, dt=F32):
            return ctx.enter_context(nc.sbuf_tensor(name, shape, dt))

        def sem(name):
            return ctx.enter_context(nc.semaphore(name))

        w_hi = sb("w_hi", [128, PIECES, 512], F32R)
        w_lo = sb("w_lo", [128, PIECES, 512], F32R)
        lin_sb = sb("lin_sb", [128, PKT, D])
        qkv = [w[:, 0:3, :].rearrange("p a n -> p (a n)").rearrange("p (k n) -> p k n", k=KT) for w in (w_hi, w_lo)]
        proj = [w[:, 3, :].rearrange("p (k n) -> p k n", k=KT) for w in (w_hi, w_lo)]
        gate_sb = sb("gate_sb", [128, KT, 128])
        NV = SEQ - 1 + 1 + 1 + 1 + 3 + 1 + EXPERTS
        vec_sb = sb("vec_sb", [128, KT, NV])
        b1_sb = sb("b1_sb", [128, MT])
        row_sb = sb("row_sb", [TT, D + 2 * EXPERTS])
        con_sb = sb("con_sb", [128, 128 + 128 + HPK + TI])
        ident = con_sb[:, 0:128]
        block_mask = con_sb[:, 128:256]
        head_mask = con_sb[:, 256:256 + HPK]
        img_mask = con_sb[0:TT, 256 + HPK:256 + HPK + TI]
        pos_raw = vec_sb[:, :, 0:SEQ - 1]
        o = SEQ - 1
        class_raw = vec_sb[:, :, o:o + 1]
        cls_raw = vec_sb[:, :, o + 1:o + 2]
        blin_raw = vec_sb[:, :, o + 2:o + 3]
        dwc = vec_sb[:, :, o + 3:o + 6]
        b_dwc = vec_sb[:, :, o + 6:o + 7]
        b2_raw = vec_sb[:, :, o + 7:o + 7 + EXPERTS]
        b_proj = row_sb[:, 0:D]
        gate_b = row_sb[:, D:D + EXPERTS]
        rms_w = row_sb[:, D + EXPERTS:D + 2 * EXPERTS]
        pos_sb = sb("pos_sb", [128, KT, PATCHES])
        w_mid = sb("w_mid", [128, KT])
        b2_sum = sb("b2_sum", [128, KT])
        neg_half = sb("neg_half", [TT, NT])

        feat_h = sb("feat_h", [128, KT, IMG, SEQ])
        tok_hb = sb("tok_hb", [TT, NT, D])
        tok_a = sb("tok_a", [TT, NT, D])
        tok_b = sb("tok_b", [TT, NT, D])
        feat_1 = sb("feat_1", [128, KT, TOK])
        feat_2 = sb("feat_2", [128, KT, TOK])
        feat_3 = sb("feat_3", [128, KT, TOK])
        att_hi = sb("att_hi", [128, KT, TOK], F32R)
        att_lo = sb("att_lo", [128, KT, TOK], F32R)
        x2_hi = sb("x2_hi", [128, KT, TOK], F32R)
        x2_lo = sb("x2_lo", [128, KT, TOK], F32R)
        g_hi = sb("g_hi", [128, SBUF_G, TOK], F32R)
        g_lo = sb("g_lo", [128, SBUF_G, TOK], F32R)
        q_spread = sb("q_spread", [128, KT, NT, TI * TT])
        v_masked = sb("v_masked", [TT, 2, KT, KVW])
        kvx = sb("kvx", [128, PKT * PTOK])
        kv_sb = kvx[:, 0:2 * KT * TI * NUMW].rearrange("p (b k i n) -> p b k i n", b=2, k=KT, i=TI)
        x_sb = kvx[:, :].rearrange("p (k n) -> p k n", k=PKT)
        wide = sb("wide", [128, 2 * NT * D + GBUF * TOK])
        tok_h2c = wide[0:TT, 0:NT * D].rearrange("p (t d) -> p t d", t=NT)
        tok_h2n = wide[0:TT, NT * D:2 * NT * D].rearrange("p (t d) -> p t d", t=NT)
        gel = wide[:, 2 * NT * D:].rearrange("p (b n) -> p b n", b=GBUF)
        stage = wide[:, 0:STAGES * 512].rearrange("p (s n) -> p s n", s=STAGES)
        stats = sb("stats", [TT, NT, 6])
        mean = sb("mean", [TT, NT])
        ls = sb("ls", [TT, 5, NT])
        var_e = sb("var_e", [TT, NT])
        rstd = sb("rstd", [TT, NT])
        k_sum = sb("k_sum", [TT, NT * HEADS])
        k_inv = sb("k_inv", [TT, NT * HEADS])
        z_inv = sb("z_inv", [TT, NT * HEADS])
        lg = sb("lg", [TT, 5, NT, EXPERTS])
        gs = sb("gs", [TT, 8, NT])
        gate_n = sb("gate_n", [TT, NT])

        ps_a = ctx.enter_context(nc.psum_tensor("ps_a", [128, 4, 512], F32))
        ps_h = ctx.enter_context(nc.psum_tensor("ps_h", [128, 2, 512], F32))
        ps_y = ctx.enter_context(nc.psum_tensor("ps_y", [128, KT, 512], F32))
        ps_tok01 = ps_a[0:TT, 0:2, :].rearrange("p b n -> p (b n)")[:, 0:NT * D].rearrange("p (t d) -> p t d", t=NT)
        ps_tok23 = ps_a[0:TT, 2:4, :].rearrange("p b n -> p (b n)")[:, 0:NT * D].rearrange("p (t d) -> p t d", t=NT)
        ps_feat01 = ps_a[:, 0:2, 0:TOK]
        ps_feat23 = ps_a[:, 2:4, 0:TOK]

        ld_small = sem("ld_small")
        ld_lin = sem("ld_lin")
        ld_x = sem("ld_x")
        ld_gate = sem("ld_gate")
        ld_stage = [sem(f"ld_stage{s}") for s in range(STAGES)]
        hi_done = [sem(f"hi_done{s}") for s in range(STAGES)]
        slot_free = [sem(f"slot_free{s}") for s in range(STAGES)]
        table = sem("table")
        zeroed_p = sem("zeroed_p")
        zeroed = sem("zeroed")
        patch_ps = sem("patch_ps")
        h_feat = sem("h_feat")
        h_tok = sem("h_tok")
        stat1 = sem("stat1")
        rstd1 = sem("rstd1")
        hb_ready = sem("hb_ready")
        xn1 = sem("xn1")
        x1_ps = sem("x1_ps")
        x1_hi = sem("x1_hi")
        x1_lo = sem("x1_lo")
        q_ps = sem("q_ps")
        q_relu = sem("q_relu")
        q_sq = sem("q_sq")
        q_cube = sem("q_cube")
        kv_ps = sem("kv_ps")
        k_relu = sem("k_relu")
        k_sq = sem("k_sq")
        k_cube = sem("k_cube")
        k_total = sem("k_total")
        k_recip = sem("k_recip")
        k_norm = sem("k_norm")
        v_ready = sem("v_ready")
        kvp_ps = sem("kvp_ps")
        kvp_sb = sem("kvp_sb")
        num_ps = sem("num_ps")
        z_ready = sem("z_ready")
        o_tok = sem("o_tok")
        o_ps = sem("o_ps")
        c_mid = sem("c_mid")
        c_add = sem("c_add")
        c_hi = sem("c_hi")
        c_lo = sem("c_lo")
        proj_ps = sem("proj_ps")
        h2_ready = sem("h2_ready")
        stat2 = sem("stat2")
        rstd2 = sem("rstd2")
        xn2 = sem("xn2")
        x2_ps = sem("x2_ps")
        x2_f = sem("x2_f")
        logit_ps = sem("logit_ps")
        gate_v = sem("gate_v")
        gate_rms = sem("gate_rms")
        gate_t = sem("gate_t")
        x2_hi_ok = sem("x2_hi_ok")
        x2_lo_ok = sem("x2_lo_ok")
        h2_moved = sem("h2_moved")
        hid_ps = sem("hid_ps")
        gelu_ok = sem("gelu_ok")
        g_hi_ok = sem("g_hi_ok")
        g_lo_ok = sem("g_lo_ok")
        y_part = sem("y_part")
        y_feat = sem("y_feat")
        y_tok = sem("y_tok")
        out_sb = sem("out_sb")
        stored = sem("stored")
        GSTEPS = 15
        LSTEPS = NT + 7
        TABLES = KT + KT + 4 + 2 * KT
        SPLIT = 2
        SPLIT_POOL = STAGES - 1

        feat_toks = [slice(SEQ * i, SEQ * i + TT) for i in TILE0]

        block = ctx.enter_context(nc.Block())

        @block.sync
        def _(sp):
            sp.dma_start(x_sb, x_p[0]).then_inc(ld_x, 16)
            sp.dma_start(lin_sb[:, :, :], w_lin).then_inc(ld_lin, 16)
            sp.dma_start(vec_sb[:, :, :], vecs).then_inc(ld_small, 16)
            sp.dma_start(con_sb[:, :], consts).then_inc(ld_small, 16)
            sp.dma_start(row_sb[:, :], rows).then_inc(ld_small, 16)
            sp.dma_start(b1_sb[:, :], b1).then_inc(ld_small, 16)
            for m in range(PIECES):
                if m >= STAGES:
                    sp.wait_ge(slot_free[m % STAGES], m // STAGES)
                sp.dma_start(stage[:, m % STAGES, :], w_pieces[m]).then_inc(ld_stage[m % STAGES], 16)
            sp.dma_start(gate_sb[:, :, :], gate_w).then_inc(ld_gate, 16)
            sp.wait_ge(num_ps, NT)
            sp.dma_start(x_sb, x_p[1]).then_inc(ld_x, 16)

            def load_next(c):
                sp.wait_ge(num_ps, (c + 1) * NT + NT)
                sp.dma_start(x_sb, x_p[c + 2]).then_inc(ld_x, 16)

            def store(c):
                sp.wait_ge(out_sb, c * NT + NT)
                sp.dma_start(out[c, 0:2 * TT, :].rearrange("(t p) d -> p t d", t=2),
                             tok_b[:, 0:2, :]).then_inc(stored, 16)
                sp.dma_start(out[c, 2 * TT:TOK, :], tok_b[3 * TT - TOK:TT, 2, :]).then_inc(stored, 16)

            with sp.Fori(0, CHUNKS - 2) as c:
                load_next(c)
                store(c)
            store(CHUNKS - 2)
            store(CHUNKS - 1)
            sp.wait_ge(stored, 32 * CHUNKS + 32)

        @block.tensor
        def _(pe):
            def patch(p, mt):
                if mt == 0:
                    pe.wait_ge(ld_x, 16 * p + 16)
                for k in range(PKT):
                    mm = pe.matmul(ps_a[:, mt, 0:PTOK], lin_sb[:, k, mt * 128:mt * 128 + 128],
                                   x_sb[:, k, :], start=(k == 0), stop=(k == PKT - 1))
                mm.then_inc(patch_ps, 1)

            def to_tok(dst, src, done):
                for t in range(NT):
                    for k in range(KT):
                        mm = pe.transpose(dst[:, t, k * 128:k * 128 + 128], src[:, k, feat_toks[t]], ident)
                mm.then_inc(done, 1)

            def to_feat(dst, src, done):
                for t in range(NT):
                    for k in range(KT):
                        mm = pe.transpose(dst[:, k, feat_toks[t]], src[:, t, k * 128:k * 128 + 128],
                                          ident[0:TT, 0:TT])
                mm.then_inc(done, 1)

            def kv_tiles(tiles):
                for t in tiles:
                    for k in range(KT):
                        for n, (x, w) in enumerate(((att_hi, qkv[0]), (att_hi, qkv[1]), (att_lo, qkv[0]))):
                            mm = pe.matmul(ps_a[0:TT, 1 + t, :], x[:, k, feat_toks[t]], w[:, k, D:3 * D],
                                           start=(k == 0 and n == 0), stop=(k == KT - 1 and n == 2))
                    mm.then_inc(kv_ps, 1)

            def q_features(mt):
                cols = slice(mt * 128, mt * 128 + 128)
                for k in range(KT):
                    for n, (w, x) in enumerate(((qkv[0], att_hi), (qkv[1], att_hi), (qkv[0], att_lo))):
                        mm = pe.matmul(ps_a[:, 0, 0:TOK], w[:, k, cols], x[:, k, :],
                                       start=(k == 0 and n == 0), stop=(k == KT - 1 and n == 2))
                mm.then_inc(q_ps, 1)

            def kv_product(a, j):
                t, k = j // KT, j % KT
                c0 = DUP if t == NT - 1 else 0
                if k == 0:
                    pe.wait_ge(v_ready, a * NT + t + 1)
                if j in (3, 4):
                    pe.wait_ge(kvp_sb, a * KVE + 2 * (j - 3) + 2)
                pe.matmul(ps_a[:, kv_bank(j), c0:KVW], tok_a[:, t, k * 128:k * 128 + 128],
                          v_masked[:, t % 2, k, c0:KVW], start=True, stop=True).then_inc(kvp_ps, 1)

            def numerators(a, t):
                pe.wait_ge(kvp_sb, a * KVE + (KVE if t == 2 else 2 * 4))
                for k in range(KT):
                    for i in range(TI):
                        kv = kv_sb[:, 1, k, TI - 1, :] if t == NT - 1 and i == 0 else kv_sb[:, t % 2, k, i, :]
                        mm = pe.matmul(ps_a[0:TT, 1 + t, k * 256:k * 256 + NUMW],
                                       q_spread[:, k, t, i * TT:i * TT + TT], kv, start=(i == 0), stop=(i == TI - 1))
                mm.then_inc(num_ps, 1)

            def attend(a, s):
                if s == 0:
                    pe.wait_ge(h_feat, a * KT + KT)
                    to_tok(ps_tok01, feat_h[:, :, :, :].rearrange("p k i s -> p k (i s)"), h_tok)
                if s == 4:
                    pe.wait_ge(xn1, a * NT + NT)
                    to_feat(ps_feat23, tok_a, x1_ps)
                if s == 6:
                    pe.wait_ge(x1_lo, a + 1)
                    pe.wait_ge(hb_ready, a + 1)
                    kv_tiles([0, 1])
                if s == 7:
                    kv_tiles([2])
                    q_features(0)
                if s == 9:
                    pe.wait_ge(q_relu, a * KT + 1)
                    q_features(1)
                if s == 11:
                    pe.wait_ge(k_norm, a + 1)
                    kv_product(a, 0)
                    pe.wait_ge(q_relu, a * KT + KT)
                    kv_product(a, 1)
                if s == 12:
                    kv_product(a, 2)
                if s == 13:
                    kv_product(a, 3)
                if s == 14:
                    kv_product(a, 4)
                    kv_product(a, 5)
                if s == 15:
                    pe.wait_ge(q_cube, a * NT + NT)
                    numerators(a, 0)
                if s == 16:
                    numerators(a, 1)
                if s == 18:
                    numerators(a, 2)
                if s == 20:
                    pe.wait_ge(o_tok, a + 1)
                    to_feat(ps_feat23, tok_a, o_ps)
                if s == 23:
                    pe.wait_ge(c_lo, a + 1)
                    for t in range(NT):
                        for k in range(KT):
                            for n, (x, w) in enumerate(((att_hi, proj[0]), (att_hi, proj[1]), (att_lo, proj[0]))):
                                mm = pe.matmul(ps_tok01[:, t, :], x[:, k, feat_toks[t]], w[:, k, :],
                                               start=(k == 0 and n == 0), stop=(k == KT - 1 and n == 2))
                    mm.then_inc(proj_ps, 1)
                if s == 28:
                    pe.wait_ge(xn2, a * NT + NT)
                    to_feat(ps_feat23, tok_a, x2_ps)
                if s == 30:
                    pe.wait_ge(x2_f, a + 1)
                    for t in range(NT):
                        for k in range(KT):
                            mm = pe.matmul(ps_a[0:TT, 3, t * 128:t * 128 + 128], feat_2[:, k, feat_toks[t]],
                                           gate_sb[:, k, :], start=(k == 0), stop=(k == KT - 1))
                    mm.then_inc(logit_ps, 1)

            def three_passes(dst, w_cols, m, hi, lo, first, last):
                for n, (w, x) in enumerate(((w_hi, hi), (w_lo, hi), (w_hi, lo))):
                    mm = pe.matmul(dst, w[:, ATT_PIECES + m, w_cols], x, start=(first and n == 0), stop=(last and n == 2))
                return mm

            def hidden(c, m):
                if m == 0:
                    pe.wait_ge(x2_lo_ok, c + 1)
                if m >= 2:
                    pe.wait_ge(gelu_ok, c * MT + m - 1)
                for k in range(KT):
                    mm = three_passes(ps_h[:, m % 2, 0:TOK], slice(k * 128, k * 128 + 128), m,
                                      x2_hi[:, k, :], x2_lo[:, k, :], k == 0, k == KT - 1)
                mm.then_inc(hid_ps, 1)

            def back(c, m):
                pe.wait_ge(g_lo_ok, c * MT + m + 1)
                for k in range(KT):
                    mm = three_passes(ps_y[:, k, 0:TOK], slice(256 + k * 128, 256 + k * 128 + 128), m,
                                      g_hi[:, m % SBUF_G, :], g_lo[:, m % SBUF_G, :], m == 0, m == MT - 1)
                mm.then_inc(y_part, 1)

            def body(c, with_attend, with_patch):
                for m in range(MT):
                    hidden(c, m)
                    if with_attend and m not in LATE:
                        attend(c + 1, m)
                    if m >= LAG:
                        back(c, m - LAG)
                    if with_attend and m in LATE:
                        attend(c + 1, m)
                if with_patch:
                    patch(c + 2, 0)
                for m in range(MT - LAG, MT):
                    back(c, m)
                if with_patch:
                    patch(c + 2, 1)
                pe.wait_ge(y_feat, c * KT + KT)
                if with_attend:
                    pe.wait_ge(gate_v, (c + 1) * GSTEPS + 1)
                to_tok(ps_tok23, feat_1, y_tok)

            pe.wait_ge(ld_lin, 16)
            for mt in range(KT):
                patch(0, mt)
            pe.wait_ge(table, TABLES)
            pe.wait_ge(zeroed, 1)
            pe.wait_ge(ld_small, 64)
            for s in range(MT):
                if s == 6:
                    for r in range(STAGES):
                        pe.wait_ge(slot_free[r], 1)
                if s == 30:
                    pe.wait_ge(ld_gate, 16)
                attend(0, s)
            for mt in range(KT):
                patch(1, mt)
            for r in range(STAGES):
                pe.wait_ge(slot_free[r], PIECES // STAGES)
            with pe.Fori(0, CHUNKS - 2) as c:
                body(c, True, True)
            body(CHUNKS - 2, True, False)
            body(CHUNKS - 1, False, False)

        @block.scalar
        def _(act):
            def attend(a, s, c=None):
                if s == 4:
                    act.wait_ge(x1_ps, a + 1)
                    act.activation(att_hi[:, :, :], ps_feat23, ACT.Copy).then_inc(x1_hi, 1)
                for t in {7: (0, 1), 8: (2,)}.get(s, ()):
                    if c is not None and t == 0:
                        act.wait_ge(stored, 32 * c + 32)
                    act.wait_ge(k_relu, a * NT + t + 1)
                    act.activation(tok_b[:, t, :], tok_a[:, t, :], ACT.Square).then_inc(k_sq, 1)
                if s in (8, 10, 12):
                    t = {8: 0, 10: 1, 12: 2}[s]
                    if t == 2:
                        act.wait_ge(kvp_ps, a * NT * KT + KT)
                    for i in range(1 if t == NT - 1 else 0, TI):
                        v = act.activation(v_masked[:, t % 2, :, i * 128:i * 128 + 128],
                                           ps_a[0:TT, 1 + t, D:2 * D].rearrange("p (k e) -> p k e", k=KT),
                                           ACT.Copy, scale=img_mask[:, i:i + 1])
                    v.then_inc(v_ready, 1)
                if s == 11:
                    act.wait_ge(q_relu, a * KT + KT)
                    act.activation(feat_3[:, :, :], feat_2[:, :, :], ACT.Square).then_inc(q_sq, 1)
                if s == 20:
                    act.wait_ge(o_ps, a + 1)
                    for k in range(KT):
                        act.activation(feat_1[:, k, :], ps_a[:, 2 + k, 0:TOK], ACT.Identity,
                                       bias=b_dwc[:, k, :], scale=w_mid[:, k:k + 1]).then_inc(c_mid, 1)
                if s == 22:
                    act.wait_ge(c_add, a * 2 * KT + 2 * KT)
                    act.activation(att_hi[:, :, :], feat_1[:, :, :], ACT.Copy).then_inc(c_hi, 1)
                if s == 29:
                    act.wait_ge(x2_ps, a + 1)
                    act.activation(feat_2[:, :, :], ps_feat23, ACT.Copy).then_inc(x2_f, 1)

            def current(c, s):
                if s == 3:
                    act.wait_ge(h2_ready, c + 1)
                    act.activation(tok_h2c, tok_h2n, ACT.Copy).then_inc(h2_moved, 1)
                if s == 6:
                    act.wait_ge(gate_v, c * GSTEPS + 8)
                    act.activation(lg[:, 2, :, :], lg[:, 1, :, :], ACT.Tanh, scale=GATE_SCALE / 2).then_inc(gate_t, 1)

            def body(c, with_attend):
                for m in range(MT):
                    act.wait_ge(hid_ps, c * MT + m + 1)
                    if m >= GBUF:
                        act.wait_ge(g_lo_ok, c * MT + m - GBUF + 1)
                    act.activation(gel[:, m % GBUF, :], ps_h[:, m % 2, 0:TOK], ACT.Gelu,
                                   bias=b1_sb[:, m:m + 1]).then_inc(gelu_ok, 1)
                    current(c, m)
                    if with_attend:
                        attend(c + 1, m, c)
                act.wait_ge(y_part, c * MT + MT)
                for k in range(KT):
                    act.activation(feat_1[:, k, :], ps_y[:, k, 0:TOK], ACT.Identity,
                                   bias=b2_sum[:, k:k + 1]).then_inc(y_feat, 1)

            act.wait_ge(ld_small, 64)
            act.wait_ge(table, TABLES)
            for s in range(MT):
                for m in range(SPLIT * s, min(SPLIT * s + SPLIT, PIECES)):
                    r = m % STAGES
                    act.wait_ge(ld_stage[r], 16 * (m // STAGES) + 16)
                    act.activation(w_hi[:, m, :], stage[:, r, :], ACT.Copy).then_inc(hi_done[r], 1)
                attend(0, s)
            with act.Fori(0, CHUNKS - 2) as c:
                body(c, True)
            body(CHUNKS - 2, True)
            body(CHUNKS - 1, False)

        @block.vector
        def _(dve):
            def f32(ap):
                return ap.bitcast(F32)

            def layer_stats(a, src, stat):
                base = a * LSTEPS
                for t in range(NT):
                    dve.bn_stats(stats[:, t, :], src[:, t, :]).then_inc(stat, 1)
                dve.wait_ge(stat, base + NT)
                dve.tensor_tensor(ls[:, 0, :], stats[:, :, 1], stats[:, :, 4], ALU.add).then_inc(stat, 1)
                dve.tensor_tensor(ls[:, 1, :], stats[:, :, 1], stats[:, :, 4], ALU.subtract).then_inc(stat, 1)
                dve.tensor_tensor(ls[:, 2, :], stats[:, :, 2], stats[:, :, 5], ALU.add).then_inc(stat, 1)
                dve.wait_ge(stat, base + NT + 3)
                dve.tensor_tensor(ls[:, 3, :], ls[:, 1, :], ls[:, 1, :], ALU.mult).then_inc(stat, 1)
                dve.tensor_scalar(ls[:, 4, :], ls[:, 2, :], 1.0 / D, LN_EPS, ALU.mult, ALU.add).then_inc(stat, 1)
                dve.tensor_scalar(mean[:, :], ls[:, 0, :], 0.5, None, ALU.mult).then_inc(stat, 1)
                dve.wait_ge(stat, base + NT + 6)
                dve.scalar_tensor_tensor(out=var_e[:, :], in0=ls[:, 3, :], scalar=0.25, in1=ls[:, 4, :],
                                         op0=ALU.mult, op1=ALU.add).then_inc(stat, 1)

            def normalise(a, src, done):
                for t in range(NT):
                    dve.tensor_scalar(tok_a[:, t, :], src[:, t, :], mean[:, t:t + 1], rstd[:, t:t + 1],
                                      ALU.subtract, ALU.mult).then_inc(done, 1)

            def kv_evacuate(a, j):
                t, k = j // KT, j % KT
                dve.wait_ge(kvp_ps, a * NT * KT + j + 1)
                first = 1 if t == NT - 1 else 0
                if j == 2 * KT:
                    dve.wait_ge(num_ps, a * NT + 1)
                ps = ps_a[:, kv_bank(j), 0:KVW]
                n = TI - first
                dve.tensor_tensor(kv_sb[:, t % 2, k, first:TI, 0:128],
                                  ps[:, first * 128:TI * 128].rearrange("p (i e) -> p i e", i=n),
                                  block_mask.unsqueeze(1).to_broadcast([128, n, 128]), ALU.mult).then_inc(kvp_sb, 1)
                dve.scalar_tensor_tensor(out=kv_sb[:, t % 2, k, first:TI, 128:NUMW],
                                         in0=ps[:, TI * 128 + first:TI * 128 + TI].unsqueeze(2)
                                         .to_broadcast([128, n, HPK]),
                                         scalar=ATT_EPS,
                                         in1=head_mask.unsqueeze(1).to_broadcast([128, n, HPK]),
                                         op0=ALU.add, op1=ALU.mult).then_inc(kvp_sb, 1)

            def attend(a, s):
                heads = lambda ap: ap.rearrange("p t (h e) -> p (t h) e", e=HD)
                if s == 0:
                    dve.wait_ge(h_tok, a + 1)
                    layer_stats(a, ps_tok01, stat1)
                if s == 2:
                    dve.wait_ge(rstd1, a + 1)
                    normalise(a, ps_tok01, xn1)
                if s == 4:
                    dve.wait_ge(x1_hi, a + 1)
                    dve.tensor_tensor(att_lo[:, :, :], ps_feat23, f32(att_hi[:, :, :]), ALU.subtract).then_inc(x1_lo, 1)
                    dve.tensor_tensor(tok_hb[:, :, :], ps_tok01,
                                      b_proj.unsqueeze(1).to_broadcast([TT, NT, D]), ALU.add).then_inc(hb_ready, 1)
                for t in {7: (0, 1), 8: (2,)}.get(s, ()):
                    dve.wait_ge(kv_ps, a * NT + t + 1)
                    dve.tensor_scalar(tok_a[:, t, :], ps_a[0:TT, 1 + t, 0:D], 0.0, ATT_EPS,
                                      ALU.max, ALU.add).then_inc(k_relu, 1)
                if s in (8, 10):
                    k = 0 if s == 8 else 1
                    dve.wait_ge(q_ps, a * KT + k + 1)
                    dve.tensor_scalar(feat_2[:, k, :], ps_a[:, 0, 0:TOK], 0.0, ATT_EPS,
                                      ALU.max, ALU.add).then_inc(q_relu, 1)
                if s == 9:
                    dve.wait_ge(k_sq, a * NT + NT)
                    dve.tensor_tensor(tok_b[:, :, :], tok_b[:, :, :], tok_a[:, :, :], ALU.mult).then_inc(k_cube, 1)
                    dve.wait_ge(k_cube, a + 1)
                    dve.tensor_reduce(k_sum[:, :], heads(tok_b[:, :, :]), AX, ALU.add).then_inc(k_total, 1)
                if s == 10:
                    dve.wait_ge(k_total, a + 1)
                    dve.reciprocal(k_inv[:, :], k_sum[:, :]).then_inc(k_recip, 1)
                    dve.wait_ge(k_recip, a + 1)
                    dve.tensor_tensor(heads(tok_a[:, :, :]), heads(tok_b[:, :, :]),
                                      k_inv[:, :].unsqueeze(2).to_broadcast([TT, NT * HEADS, HD]),
                                      ALU.mult).then_inc(k_norm, 1)
                if s == 12:
                    kv_evacuate(a, 0)
                    kv_evacuate(a, 1)
                    dve.wait_ge(q_sq, a + 1)
                    for t in range(NT):
                        dve.tensor_tensor(spread(q_spread, t),
                                          feat_3[:, :, feat_toks[t]].rearrange("p k (i s) -> p k i s", i=TI),
                                          feat_2[:, :, feat_toks[t]].rearrange("p k (i s) -> p k i s", i=TI),
                                          ALU.mult).then_inc(q_cube, 1)
                if s == 13:
                    kv_evacuate(a, 2)
                if s == 14:
                    kv_evacuate(a, 3)
                if s == 16:
                    kv_evacuate(a, 4)
                    kv_evacuate(a, 5)
                if s == 19:
                    dve.wait_ge(num_ps, a * NT + NT)
                    halves = ps_a[0:TT, 1:4, :].rearrange("p t (k n) -> p (t k) n", k=KT)
                    z = z_inv[:, :].rearrange("p (g h) -> p g h", h=HPK)
                    dve.reciprocal(z, halves[:, :, 128:NUMW]).then_inc(z_ready, 1)
                    dve.wait_ge(z_ready, a + 1)
                    dve.tensor_tensor(tok_a[:, :, :].rearrange("p t (k h e) -> p (t k) h e", k=KT, e=HD),
                                      halves[:, :, 0:128].rearrange("p g (h e) -> p g h e", e=HD),
                                      z.unsqueeze(3).to_broadcast([TT, NT * KT, HPK, HD]), ALU.mult).then_inc(o_tok, 1)
                if s == 21:
                    o_img = ps_feat23.rearrange("p k (i s) -> p k i s", s=SEQ)
                    c_img = feat_1[:, :, :].rearrange("p k (i s) -> p k i s", s=SEQ)
                    for side in range(2):
                        for k in range(KT):
                            dst = c_img[:, k, :, 1:SEQ] if side == 0 else c_img[:, k, :, 0:SEQ - 1]
                            src = o_img[:, k, :, 0:SEQ - 1] if side == 0 else o_img[:, k, :, 1:SEQ]
                            if side == 0:
                                dve.wait_ge(c_mid, a * KT + k + 1)
                            else:
                                dve.wait_ge(c_add, a * 2 * KT + k + 1)
                            dve.scalar_tensor_tensor(out=dst, in0=src, scalar=dwc[:, k, 2 * side:2 * side + 1],
                                                     in1=dst, op0=ALU.mult, op1=ALU.add).then_inc(c_add, 1)
                if s == 22:
                    dve.wait_ge(c_hi, a + 1)
                    dve.tensor_tensor(att_lo[:, :, :], feat_1[:, :, :], f32(att_hi[:, :, :]),
                                      ALU.subtract).then_inc(c_lo, 1)
                if s == 24:
                    dve.wait_ge(proj_ps, a + 1)
                    dve.wait_ge(h2_moved, a)
                    dve.wait_ge(hb_ready, a + 1)
                    dve.tensor_tensor(tok_h2n, ps_tok01, tok_hb[:, :, :], ALU.add).then_inc(h2_ready, 1)
                    dve.wait_ge(h2_ready, a + 1)
                    layer_stats(a, tok_h2n, stat2)
                if s == 27:
                    dve.wait_ge(rstd2, a + 1)
                    normalise(a, tok_h2n, xn2)

            def add_gate_bias(a):
                dve.wait_ge(logit_ps, a + 1)
                logits = ps_a[0:TT, 3, 0:NT * 128].rearrange("p (t n) -> p t n", t=NT)[:, :, 0:EXPERTS]
                dve.tensor_tensor(lg[:, 0, :, :], logits,
                                  gate_b.unsqueeze(1).to_broadcast([TT, NT, EXPERTS]), ALU.add).then_inc(gate_v, 1)

            def current(a, s):
                if s == 1:
                    dve.wait_ge(gate_v, a * GSTEPS + 1)
                    dve.tensor_tensor(lg[:, 1, :, :], lg[:, 0, :, :], lg[:, 0, :, :], ALU.mult).then_inc(gate_v, 1)
                    dve.wait_ge(gate_v, a * GSTEPS + 2)
                    dve.tensor_reduce(gs[:, 0, :], lg[:, 1, :, :], AX, ALU.add).then_inc(gate_v, 1)
                    dve.wait_ge(gate_v, a * GSTEPS + 3)
                    dve.tensor_scalar(gs[:, 1, :], gs[:, 0, :], 1.0 / EXPERTS, RMS_EPS,
                                      ALU.mult, ALU.add).then_inc(gate_v, 1)
                if s == 5:
                    dve.wait_ge(gate_rms, a + 1)
                    dve.tensor_tensor(lg[:, 3, :, :], lg[:, 0, :, :],
                                      gs[:, 2, :].unsqueeze(2).to_broadcast([TT, NT, EXPERTS]),
                                      ALU.mult).then_inc(gate_v, 1)
                    dve.wait_ge(gate_v, a * GSTEPS + 5)
                    dve.tensor_tensor(lg[:, 4, :, :], lg[:, 3, :, :],
                                      rms_w.unsqueeze(1).to_broadcast([TT, NT, EXPERTS]), ALU.mult).then_inc(gate_v, 1)
                    dve.wait_ge(gate_v, a * GSTEPS + 6)
                    dve.tensor_reduce(gs[:, 3, :], lg[:, 4, :, :], AX, ALU.max).then_inc(gate_v, 1)
                    dve.wait_ge(gate_v, a * GSTEPS + 7)
                    dve.tensor_tensor(lg[:, 1, :, :], lg[:, 4, :, :],
                                      gs[:, 3, :].unsqueeze(2).to_broadcast([TT, NT, EXPERTS]),
                                      ALU.subtract).then_inc(gate_v, 1)
                if s == 7:
                    gate_end(a)

            def gate_end(a):
                dve.wait_ge(gate_t, a + 1)
                dve.tensor_scalar(lg[:, 0, :, :], lg[:, 2, :, :], 1.0, None, ALU.add).then_inc(gate_v, 1)
                dve.tensor_scalar(lg[:, 3, :, :], lg[:, 2, :, :], -1.0, 1.0, ALU.mult, ALU.add).then_inc(gate_v, 1)
                dve.wait_ge(gate_v, a * GSTEPS + 10)
                dve.reciprocal(lg[:, 4, :, :], lg[:, 3, :, :]).then_inc(gate_v, 1)
                dve.wait_ge(gate_v, a * GSTEPS + 11)
                dve.tensor_tensor(lg[:, 1, :, :], lg[:, 0, :, :], lg[:, 4, :, :], ALU.mult).then_inc(gate_v, 1)
                dve.wait_ge(gate_v, a * GSTEPS + 12)
                dve.tensor_reduce(gs[:, 4, :], lg[:, 1, :, :], AX, ALU.add).then_inc(gate_v, 1)
                dve.wait_ge(gate_v, a * GSTEPS + 13)
                dve.tensor_scalar(gs[:, 5, :], gs[:, 4, :], NORM_EPS, 1.0, ALU.mult, ALU.add).then_inc(gate_v, 1)
                dve.wait_ge(gate_v, a * GSTEPS + 14)
                dve.reciprocal(gate_n[:, :], gs[:, 5, :]).then_inc(gate_v, 1)

            def split_input(a, running):
                dve.wait_ge(x2_f, a + 1)
                if running:
                    dve.wait_ge(hid_ps, a * MT)
                dve.tensor_copy(x2_hi[:, :, :], feat_2[:, :, :]).then_inc(x2_hi_ok, 1)
                dve.wait_ge(x2_hi_ok, a + 1)
                dve.tensor_tensor(x2_lo[:, :, :], feat_2[:, :, :], f32(x2_hi[:, :, :]),
                                  ALU.subtract).then_inc(x2_lo_ok, 1)

            def add_position(p):
                for k in range(KT):
                    dve.wait_ge(patch_ps, p * KT + k + 1)
                    dve.tensor_tensor(feat_h[:, k, :, 2:SEQ],
                                      ps_a[:, k, 0:PTOK].rearrange("p (i s) -> p i s", i=IMG),
                                      pos_sb[:, k, :].unsqueeze(1).to_broadcast([128, IMG, PATCHES]),
                                      ALU.add).then_inc(h_feat, 1)

            def body(c, with_attend, with_patch):
                for m in range(MT):
                    dve.wait_ge(gelu_ok, c * MT + m + 1)
                    if m >= SBUF_G:
                        dve.wait_ge(y_part, c * MT + m - SBUF_G + 1)
                    dve.tensor_copy(g_hi[:, m % SBUF_G, :], gel[:, m % GBUF, :]).then_inc(g_hi_ok, 1)
                    dve.wait_ge(g_hi_ok, c * MT + m + 1)
                    dve.tensor_tensor(g_lo[:, m % SBUF_G, :], gel[:, m % GBUF, :], f32(g_hi[:, m % SBUF_G, :]),
                                      ALU.subtract).then_inc(g_lo_ok, 1)
                    current(c, m)
                    if with_attend:
                        attend(c + 1, m)
                if with_attend:
                    split_input(c + 1, True)
                    add_gate_bias(c + 1)
                if with_patch:
                    add_position(c + 2)
                dve.wait_ge(y_tok, c + 1)
                dve.wait_ge(h2_moved, c + 1)
                dve.wait_ge(gate_v, c * GSTEPS + GSTEPS)
                dve.wait_ge(stored, 32 * c + 32)
                for t in range(NT):
                    dve.scalar_tensor_tensor(out=tok_b[:, t, :], in0=ps_tok23[:, t, :], scalar=gate_n[:, t:t + 1],
                                             in1=tok_h2c[:, t, :], op0=ALU.mult, op1=ALU.add).then_inc(out_sb, 1)

            dve.wait_ge(ld_small, 64)
            for k in range(KT):
                dve.tensor_scalar(pos_sb[:, k, :], pos_raw[:, k, 1:SEQ - 1], blin_raw[:, k, :], None,
                                  ALU.add).then_inc(table, 1)
            for k in range(KT):
                dve.tensor_scalar(feat_h[:, k, :, 1], class_raw[:, k, :].to_broadcast([128, IMG]),
                                  pos_raw[:, k, 0:1], None, ALU.add).then_inc(table, 1)
            dve.tensor_copy(feat_h[:, 0, :, 0], cls_raw[:, 0, :].to_broadcast([128, IMG])).then_inc(table, 1)
            dve.tensor_copy(feat_h[:, 1, :, 0], cls_raw[:, 1, :].to_broadcast([128, IMG])).then_inc(table, 1)
            dve.tensor_scalar(w_mid[:, :], dwc[:, :, 1], 1.0, None, ALU.add).then_inc(table, 1)
            dve.tensor_reduce(b2_sum[:, :], b2_raw, AX, ALU.add).then_inc(table, 1)
            for b in range(2):
                for k in range(KT):
                    dve.tensor_copy(v_masked[:, b, k, TI * 128:KVW], img_mask).then_inc(table, 1)
            dve.wait_ge(table, TABLES)
            dve.wait_ge(zeroed, 1)
            add_position(0)
            for s in range(MT):
                for m in range(SPLIT * s, min(SPLIT * s + SPLIT, PIECES)):
                    r = m % STAGES
                    if r != SPLIT_POOL:
                        dve.wait_ge(hi_done[r], m // STAGES + 1)
                        dve.tensor_tensor(w_lo[:, m, :], stage[:, r, :], f32(w_hi[:, m, :]),
                                          ALU.subtract).then_inc(slot_free[r], 1)
                if s == 24:
                    dve.wait_ge(slot_free[SPLIT_POOL], PIECES // STAGES)
                attend(0, s)
            split_input(0, False)
            add_gate_bias(0)
            add_position(1)
            with dve.Fori(0, CHUNKS - 2) as c:
                body(c, True, True)
            body(CHUNKS - 2, True, False)
            body(CHUNKS - 1, False, False)

        @block.gpsimd
        def _(pool):
            pool.memset(q_spread[:, :, :, :], 0.0).then_inc(zeroed_p, 1)
            pool.memset(neg_half[:, :], -0.5).then_inc(zeroed_p, 1)
            pool.wait_ge(zeroed_p, 2)
            pool.sem_inc(zeroed, 1)
            pool.sem_inc(stored, 32)

            def power(dst, src, done):
                pool.tensor_tensor(dst, src, neg_half[:, :], ALU.pow).then_inc(done, 1)

            def split_lo(pieces):
                for m in pieces:
                    r = m % STAGES
                    if r == SPLIT_POOL:
                        pool.wait_ge(hi_done[r], m // STAGES + 1)
                        pool.tensor_tensor(w_lo[:, m, :], stage[:, r, :], w_hi[:, m, :].bitcast(F32),
                                           ALU.subtract).then_inc(slot_free[r], 1)

            def norm1(a):
                pool.wait_ge(stat1, a * LSTEPS + LSTEPS)
                power(rstd[:, :], var_e[:, :], rstd1)

            def norm2(a):
                pool.wait_ge(stat2, a * LSTEPS + LSTEPS)
                power(rstd[:, :], var_e[:, :], rstd2)

            def gate(a):
                pool.wait_ge(gate_v, a * GSTEPS + 4)
                power(gs[:, 2, :], gs[:, 1, :], gate_rms)

            norm1(0)
            split_lo(range(PIECES))
            norm2(0)
            with pool.Fori(0, CHUNKS - 1) as c:
                norm1(c + 1)
                gate(c)
                norm2(c + 1)
            gate(CHUNKS - 1)


def kernel(**inputs):
    import numpy as np
    import concourse.bacc as bacc
    from concourse.bass_utils import run_bass_kernel_spmd

    g = {n: np.asarray(v) for n, v in inputs.items()}

    def rows_on_partitions(w):
        return w.reshape(-1, 128, w.shape[-1]).transpose(1, 0, 2)

    x = g["x"].reshape(CHUNKS, IMG, CHAN, GRID, PATCH, GRID, PATCH).transpose(0, 2, 4, 6, 1, 3, 5)
    x = x.reshape(CHUNKS, PKT, 128, PTOK).transpose(0, 2, 1, 3)
    gate = np.zeros((D, 128), g["L0_ffn_gate_w"].dtype)
    gate[:, :EXPERTS] = g["L0_ffn_gate_w"].T
    qkv = rows_on_partitions(g["L0_attn_w_qkv"].T).reshape(128, -1, 512).transpose(1, 0, 2)
    proj = rows_on_partitions(g["L0_attn_w_proj"].T).reshape(128, -1, 512).transpose(1, 0, 2)
    w1 = g["L0_ffn_w1"].transpose(1, 0, 2).reshape(KT, 128, MT, 128).transpose(2, 1, 0, 3).reshape(MT, 128, D)
    w2 = g["L0_ffn_w2"].reshape(MT, 128, D)
    vecs = np.concatenate([g["L0_tok_position_embeddings"][0].T, g["L0_tok_class_token"][0].T, g["cls_tok"][0].T,
                           g["L0_tok_b_lin"][:, None], g["L0_attn_w_dwc"], g["L0_attn_b_dwc"][:, None],
                           g["L0_ffn_b2"].T], axis=1)
    rows = np.concatenate([g["L0_attn_b_proj"], g["L0_ffn_gate_b"], g["L0_ffn_rms_w"]])
    heads = np.arange(128) // HD
    consts = np.concatenate([np.eye(128), heads[:, None] == heads[None, :],
                             heads[:, None] == np.arange(HPK)[None, :],
                             np.arange(128)[:, None] // SEQ == np.arange(TI)[None, :]], axis=1).astype(np.float32)
    sent = {
        "x_p": x,
        "w_lin": rows_on_partitions(g["L0_tok_W_lin"].T),
        "gate_w": rows_on_partitions(gate),
        "w_pieces": np.concatenate([qkv, proj, np.concatenate([w1, w2], axis=2)]),
        "vecs": rows_on_partitions(vecs),
        "b1": g["L0_ffn_b1"].reshape(MT, 128).T,
        "rows": np.broadcast_to(rows, (TT, rows.size)),
        "consts": consts,
    }
    nc = bacc.Bacc("TRN2", target_bir_lowering=False, num_devices=1, dynamic_dma_scratch_size=1024)
    sent = {n: np.ascontiguousarray(v) for n, v in sent.items()}
    args = {n: nc.dram_tensor(n, v.shape, mybir.dt.from_np(v.dtype), kind="ExternalInput").ap() for n, v in sent.items()}
    out = nc.dram_tensor("out", (IMAGES, SEQ, D), F32, kind="ExternalOutput").ap()
    vit_block(nc, out=out.rearrange("(c i) s d -> c (i s) d", c=CHUNKS), **args)
    r = run_bass_kernel_spmd(nc, [sent], core_ids=[0])
    return r.results[0]["out"]
```

```python
from contextlib import ExitStack

import concourse.bass as bass
from concourse import mybir

F32 = mybir.dt.float32
F32R = mybir.dt.float32r
ALU = mybir.AluOpType
ACT = mybir.ActivationFunctionType
AX = mybir.AxisListType.X

IMAGES, CHAN, SIDE, PATCH = 64, 3, 96, 16
GRID = SIDE // PATCH
PATCHES = GRID * GRID
SEQ = PATCHES + 2
D = 256
KT = D // 128
PIX = CHAN * PATCH * PATCH
PKT = PIX // 128
HEADS, HD = 16, 16
EXPERTS, HID = 8, 512
MT = EXPERTS * HID // 128
ATT_PIECES = 4
PIECES = ATT_PIECES + MT

CHUNKS = 8
IMG = IMAGES // CHUNKS
TOK = IMG * SEQ
PTOK = IMG * PATCHES
TI = 3
TT = TI * SEQ
TILE0 = [0, 3, 5]
NT = len(TILE0)
HPK = 128 // HD
KVW = TI * 128 + TI
DUP = 128
KVE = 2 * NT * KT
NUMW = 128 + HPK

ATT_EPS = 1e-6
LN_EPS = 1e-5
RMS_EPS = 1.1920928955078125e-07
GATE_SCALE = 2.0
NORM_EPS = 1e-6
TINY = 1e-30

GBUF = 2
SBUF_G = 4
LAG = 3
EARLY = (0,)
LATE = (4, 6, 17, 18, 22, 26, 31)
FIRST_PARTS = [range(0, 1), range(1, 3), range(3, PKT)]
LOADS = (4, 4, 4, 8, 16)
KEEP_CLOCK = {0: 1, 4: 9, 22: 4, 26: 8, 31: 8}
SPLIT_X = {27: (0,), 28: (1, 2), 29: (3, 4), 30: (5,)}
POOL_ATT = 2
FIRST_LO = MT // 2
SPLIT_HI = {0: 2, 1: 2, 4: 4, 11: 4, 15: 4, 18: 4, 24: 6, 26: 6}


def load_of(m):
    return next(i for i in range(len(LOADS)) if m < sum(LOADS[:i + 1]))


def kv_bank(j):
    return (1, 0, 2, 1, 0, 3)[j]


def spread(q, t):
    ap = q[:, :, t, :]
    (pitch, parts), (k_step, k_n), _ = ap.ap
    return bass.AP(ap.tensor, ap.offset, [[pitch, parts], [k_step, k_n], [TT + SEQ, TI], [1, SEQ]])


def vit_block(nc, x_p, w_lin, gate_w, w_pieces, vecs, b1, rows, consts, out):
    with ExitStack() as ctx:
        def sb(name, shape, dt=F32):
            return ctx.enter_context(nc.sbuf_tensor(name, shape, dt))

        def under(name, shape, dt=F32):
            with nc.sbuf_tensor(name, shape, dt) as t:
                return t

        def sem(name):
            return ctx.enter_context(nc.semaphore(name))

        w_hi = sb("w_hi", [128, PIECES, 512], F32R)
        w_raw = under("w_raw", [128, PIECES, 512])
        w_lo = sb("w_lo", [128, PIECES, 512], F32R)
        lin_hi = sb("lin_hi", [128, PKT, D], F32R)
        lin_raw = under("lin_raw", [128, PKT, D])
        lin_lo = sb("lin_lo", [128, PKT, D], F32R)
        qkv = [w[:, 0:3, :].rearrange("p a n -> p (a n)").rearrange("p (k n) -> p k n", k=KT) for w in (w_hi, w_lo)]
        proj = [w[:, 3, :].rearrange("p (k n) -> p k n", k=KT) for w in (w_hi, w_lo)]
        gate_sb = sb("gate_sb", [128, KT, 128])
        NV = SEQ - 1 + 1 + 1 + 1 + 3 + 1 + EXPERTS
        vec_sb = sb("vec_sb", [128, KT, NV])
        b1_sb = sb("b1_sb", [128, MT])
        row_sb = sb("row_sb", [TT, D + 2 * EXPERTS])
        con_sb = sb("con_sb", [128, 128 + 128 + HPK + TI])
        ident = con_sb[:, 0:128]
        block_mask = con_sb[:, 128:256]
        head_mask = con_sb[:, 256:256 + HPK]
        img_mask = con_sb[0:TT, 256 + HPK:256 + HPK + TI]
        pos_raw = vec_sb[:, :, 0:SEQ - 1]
        o = SEQ - 1
        class_raw = vec_sb[:, :, o:o + 1]
        cls_raw = vec_sb[:, :, o + 1:o + 2]
        blin_raw = vec_sb[:, :, o + 2:o + 3]
        dwc = vec_sb[:, :, o + 3:o + 6]
        b_dwc = vec_sb[:, :, o + 6:o + 7]
        b2_raw = vec_sb[:, :, o + 7:o + 7 + EXPERTS]
        b_proj = row_sb[:, 0:D]
        gate_b = row_sb[:, D:D + EXPERTS]
        rms_w = row_sb[:, D + EXPERTS:D + 2 * EXPERTS]
        pos_sb = sb("pos_sb", [128, KT, PATCHES])
        w_mid = sb("w_mid", [128, KT])
        b2_sum = sb("b2_sum", [128, KT])
        neg_half = sb("neg_half", [TT, NT])

        feat_h = sb("feat_h", [128, KT, IMG, SEQ])
        tok_hb = sb("tok_hb", [TT, NT, D])
        tok_a = sb("tok_a", [TT, NT, D])
        feat_1 = sb("feat_1", [128, KT, TOK])
        feat_2 = sb("feat_2", [128, KT, TOK])
        x_hi = under("x_hi", [128, PKT, PTOK], F32R)
        att_hi = sb("att_hi", [128, KT, TOK], F32R)
        att_lo = sb("att_lo", [128, KT, TOK], F32R)
        tok_b = sb("tok_b", [TT, NT, D])
        x2_hi = sb("x2_hi", [128, KT, TOK], F32R)
        x2_lo = sb("x2_lo", [128, KT, TOK], F32R)
        g_hi = sb("g_hi", [128, SBUF_G, TOK], F32R)
        g_lo = sb("g_lo", [128, SBUF_G, TOK], F32R)
        q_spread = sb("q_spread", [128, KT, NT, TI * TT])
        tok_h2n = under("tok_h2n", [TT, NT, D])
        v_masked = sb("v_masked", [TT, 2, KT, KVW])
        kv_sb = under("kv_sb", [128, 2, KT, TI, NUMW])
        x_raw = under("x_raw", [128, PKT, PTOK])
        x_lo = sb("x_lo", [128, PKT, PTOK], F32R)
        tok_h2c = sb("tok_h2c", [TT, NT, D])
        gel = sb("gel", [128, GBUF, TOK])
        stats = sb("stats", [TT, NT, 6])
        mean = sb("mean", [TT, NT])
        ls = sb("ls", [TT, 5, NT])
        var_e = sb("var_e", [TT, NT])
        rstd = sb("rstd", [TT, NT])
        k_sum = sb("k_sum", [TT, NT * HEADS])
        k_inv = sb("k_inv", [TT, NT * HEADS])
        z_inv = sb("z_inv", [TT, NT * HEADS])
        den = k_sum
        lg = sb("lg", [TT, 5, NT, EXPERTS])
        gs = sb("gs", [TT, 8, NT])
        gate_n = sb("gate_n", [TT, NT])

        ps_a = ctx.enter_context(nc.psum_tensor("ps_a", [128, 4, 512], F32))
        ps_h = ctx.enter_context(nc.psum_tensor("ps_h", [128, 2, 512], F32))
        ps_y = ctx.enter_context(nc.psum_tensor("ps_y", [128, KT, 512], F32))
        ps_tok01 = ps_a[0:TT, 0:2, :].rearrange("p b n -> p (b n)")[:, 0:NT * D].rearrange("p (t d) -> p t d", t=NT)
        ps_tok23 = ps_a[0:TT, 2:4, :].rearrange("p b n -> p (b n)")[:, 0:NT * D].rearrange("p (t d) -> p t d", t=NT)
        ps_feat01 = ps_a[:, 0:2, 0:TOK]
        ps_feat23 = ps_a[:, 2:4, 0:TOK]

        ld_small = sem("ld_small")
        ld_x0 = [sem(f"ld_x0_{h}") for h in range(len(FIRST_PARTS))]
        ld_x = sem("ld_x")
        lin_hi_ok = sem("lin_hi_ok")
        lin_lo_ok = sem("lin_lo_ok")
        x_hi_ok = sem("x_hi_ok")
        x_lo_ok = sem("x_lo_ok")
        ld_rows = sem("ld_rows")
        ld_gate = sem("ld_gate")
        ld_w = [sem(f"ld_w{i}") for i in range(len(LOADS))]
        w_hi_ok = sem("w_hi_ok")
        att_lo_ok = sem("att_lo_ok")
        att_pool_ok = sem("att_pool_ok")
        w_lo_ok = sem("w_lo_ok")
        table = sem("table")
        zeroed_p = sem("zeroed_p")
        zeroed = sem("zeroed")
        blank = sem("blank")
        patch_ps = sem("patch_ps")
        h_feat = sem("h_feat")
        h_tok = sem("h_tok")
        stat1 = sem("stat1")
        rstd1 = sem("rstd1")
        hb_ready = sem("hb_ready")
        xn1 = sem("xn1")
        x1_ps = sem("x1_ps")
        x1_hi = sem("x1_hi")
        x1_lo = sem("x1_lo")
        q_ps = sem("q_ps")
        q_relu = sem("q_relu")
        q_sq = sem("q_sq")
        q_cube = sem("q_cube")
        kv_ps = sem("kv_ps")
        k_relu = sem("k_relu")
        k_sq = sem("k_sq")
        k_cube = sem("k_cube")
        k_total = sem("k_total")
        k_recip = sem("k_recip")
        k_norm = sem("k_norm")
        masks_ok = sem("masks_ok")
        v_ready = sem("v_ready")
        kvp_ps = sem("kvp_ps")
        kvp_sb = sem("kvp_sb")
        num_ps = sem("num_ps")
        den_ok = sem("den_ok")
        z_ready = sem("z_ready")
        o_tok = sem("o_tok")
        o_ps = sem("o_ps")
        c_mid = sem("c_mid")
        c_add = sem("c_add")
        c_hi = sem("c_hi")
        c_lo = sem("c_lo")
        proj_ps = sem("proj_ps")
        h2_ready = sem("h2_ready")
        stat2 = sem("stat2")
        rstd2 = sem("rstd2")
        xn2 = sem("xn2")
        x2_ps = sem("x2_ps")
        x2_f = sem("x2_f")
        logit_ps = sem("logit_ps")
        gate_v = sem("gate_v")
        gate_rms = sem("gate_rms")
        gate_t = sem("gate_t")
        x2_hi_ok = sem("x2_hi_ok")
        x2_lo_ok = sem("x2_lo_ok")
        h2_moved = sem("h2_moved")
        hid_ps = sem("hid_ps")
        gelu_ok = sem("gelu_ok")
        g_hi_ok = sem("g_hi_ok")
        g_lo_ok = sem("g_lo_ok")
        y_part = sem("y_part")
        y_done = sem("y_done")
        y_feat = sem("y_feat")
        y_tok = sem("y_tok")
        out_sb = sem("out_sb")
        stored = sem("stored")
        GSTEPS = 15
        LSTEPS = NT + 7
        TABLES = KT + KT + 4 + KT

        feat_toks = [slice(SEQ * i, SEQ * i + TT) for i in TILE0]

        def load_lin(queue, h):
            ks = slice(FIRST_PARTS[h].start, FIRST_PARTS[h].stop)
            queue.dma_start(lin_raw[:, ks, :], w_lin[:, ks, :]).then_inc(ld_x0[h], 16)

        block = ctx.enter_context(nc.Block())

        @block.sync
        def _(sp):
            for h, ks in enumerate(FIRST_PARTS):
                sp.dma_start(x_raw[:, ks.start:ks.stop, :], x_p[0][:, ks.start:ks.stop, :]).then_inc(ld_x0[h], 16)
                if h > 0:
                    load_lin(sp, h)
            first = 0
            for i, n in enumerate(LOADS):
                if i == 1:
                    sp.dma_start(row_sb[:, :], rows).then_inc(ld_rows, 16)
                    sp.dma_start(b1_sb[:, :], b1).then_inc(ld_rows, 16)
                if i == 2:
                    sp.wait_ge(patch_ps, KT)
                    sp.dma_start(x_raw[:, :, :], x_p[1]).then_inc(ld_x, 16)
                sp.dma_start(w_raw[:, first:first + n, :], w_pieces[:, first:first + n, :]).then_inc(ld_w[i], 16)
                first += n
            sp.dma_start(gate_sb[:, :, :], gate_w).then_inc(ld_gate, 16)

            def load_next(c):
                sp.wait_ge(num_ps, (c + 1) * NT + NT)
                sp.dma_start(x_raw[:, :, :], x_p[c + 2]).then_inc(ld_x, 16)

            def store(c):
                sp.wait_ge(out_sb, c * NT + 2)
                sp.dma_start(out[c, 0:2 * TT, :].rearrange("(t p) d -> p t d", t=2),
                             tok_b[:, 0:2, :]).then_inc(stored, 16)
                sp.wait_ge(out_sb, c * NT + NT)
                sp.dma_start(out[c, 2 * TT:TOK, :], tok_b[3 * TT - TOK:TT, 2, :]).then_inc(stored, 16)

            with sp.Fori(0, CHUNKS - 2) as c:
                load_next(c)
                store(c)
            store(CHUNKS - 2)
            store(CHUNKS - 1)
            sp.wait_ge(stored, 32 * CHUNKS + 32)

        @block.tensor
        def _(pe):
            def patch_1(mt):
                if mt == 0:
                    pe.wait_ge(ld_x, 16)
                for k in range(PKT):
                    mm = pe.matmul(ps_h[:, mt, 0:PTOK], lin_raw[:, k, mt * 128:mt * 128 + 128],
                                   x_raw[:, k, :], start=(k == 0), stop=(k == PKT - 1))
                mm.then_inc(patch_ps, 1)

            def patch(p, mt):
                for k in range(PKT):
                    if mt == 0:
                        pe.wait_ge(x_lo_ok, (p - 2) * PKT + k + 1)
                    for n, (w, x) in enumerate(((lin_hi, x_hi), (lin_lo, x_hi), (lin_hi, x_lo))):
                        mm = pe.matmul(ps_a[:, mt, 0:PTOK], w[:, k, mt * 128:mt * 128 + 128], x[:, k, :],
                                       start=(k == 0 and n == 0), stop=(k == PKT - 1 and n == 2))
                mm.then_inc(patch_ps, 1)

            def to_tok(dst, src, done, ready=None, before=0):
                for k in range(KT):
                    if ready is not None:
                        pe.wait_ge(ready, before + k + 1)
                    for t in range(NT):
                        mm = pe.transpose(dst[:, t, k * 128:k * 128 + 128], src[:, k, feat_toks[t]], ident)
                mm.then_inc(done, 1)

            def to_feat(a, dst, src, ready, per, done, tiles=range(NT)):
                for t in tiles:
                    if per == NT or t == tiles[0]:
                        pe.wait_ge(ready, a * per + (t if per == NT else 0) + 1)
                    for k in range(KT):
                        mm = pe.transpose(dst[:, k, feat_toks[t]], src[:, t, k * 128:k * 128 + 128],
                                          ident[0:TT, 0:TT])
                mm.then_inc(done, 1)

            def kv_tiles(tiles):
                for t in tiles:
                    for k in range(KT):
                        for n, (x, w) in enumerate(((att_hi, qkv[0]), (att_hi, qkv[1]), (att_lo, qkv[0]))):
                            mm = pe.matmul(ps_a[0:TT, 1 + t, :], x[:, k, feat_toks[t]], w[:, k, D:3 * D],
                                           start=(k == 0 and n == 0), stop=(k == KT - 1 and n == 2))
                    mm.then_inc(kv_ps, 1)

            def q_features(mt):
                cols = slice(mt * 128, mt * 128 + 128)
                for k in range(KT):
                    for n, (w, x) in enumerate(((qkv[0], att_hi), (qkv[1], att_hi), (qkv[0], att_lo))):
                        mm = pe.matmul(ps_a[:, 0, 0:TOK], w[:, k, cols], x[:, k, :],
                                       start=(k == 0 and n == 0), stop=(k == KT - 1 and n == 2))
                mm.then_inc(q_ps, 1)

            def kv_product(a, j):
                t, k = j // KT, j % KT
                c0 = DUP if t == NT - 1 else 0
                if k == 0:
                    pe.wait_ge(v_ready, a * NT + t + 1)
                if j in (3, 4):
                    pe.wait_ge(kvp_sb, a * KVE + 2 * (j - 3) + 2)
                pe.matmul(ps_a[:, kv_bank(j), c0:KVW], tok_a[:, t, k * 128:k * 128 + 128],
                          v_masked[:, t % 2, k, c0:KVW], start=True, stop=True).then_inc(kvp_ps, 1)

            def numerators(a, t):
                pe.wait_ge(kvp_sb, a * KVE + (KVE if t == 2 else 2 * 4))
                first = 1 if t == NT - 1 else 0
                for k in range(KT):
                    for i in range(first, TI):
                        mm = pe.matmul(ps_a[0:TT, 1 + t, k * 256:k * 256 + NUMW],
                                       q_spread[:, k, t, i * TT:i * TT + TT], kv_sb[:, t % 2, k, i, :],
                                       start=(i == first), stop=(i == TI - 1))
                mm.then_inc(num_ps, 1)

            def attend(a, s):
                if s == 0:
                    pe.wait_ge(h_feat, a * KT + KT)
                    to_tok(ps_tok01, feat_h[:, :, :, :].rearrange("p k i s -> p k (i s)"), h_tok)
                if s == 4:
                    to_feat(a, ps_feat23, tok_a, xn1, NT, x1_ps)
                if s == 6:
                    pe.wait_ge(x1_lo, a * KT + KT)
                    pe.wait_ge(hb_ready, a + 1)
                    kv_tiles([0, 1])
                if s == 7:
                    kv_tiles([2])
                    q_features(0)
                if s == 10:
                    pe.wait_ge(q_relu, a * KT + 1)
                    q_features(1)
                if s == 14:
                    pe.wait_ge(k_norm, a + 1)
                    pe.wait_ge(masks_ok, a + 1)
                    kv_product(a, 0)
                    pe.wait_ge(q_relu, a * KT + KT)
                    kv_product(a, 1)
                if s == 15:
                    kv_product(a, 2)
                if s == 16:
                    kv_product(a, 3)
                    kv_product(a, 4)
                    kv_product(a, 5)
                if s == 17:
                    pe.wait_ge(q_cube, a * NT + NT)
                    numerators(a, 0)
                if s == 18:
                    numerators(a, 1)
                if s == 19:
                    numerators(a, 2)
                if s == 22:
                    to_feat(a, ps_feat23, tok_a, o_tok, 1, o_ps, (0, 2, 1))
                if s == 26:
                    pe.wait_ge(c_lo, a * KT + KT)
                    for t in range(NT):
                        for k in range(KT):
                            for n, (x, w) in enumerate(((att_hi, proj[0]), (att_hi, proj[1]), (att_lo, proj[0]))):
                                mm = pe.matmul(ps_tok01[:, t, :], x[:, k, feat_toks[t]], w[:, k, :],
                                               start=(k == 0 and n == 0), stop=(k == KT - 1 and n == 2))
                        if t >= NT - 2:
                            mm.then_inc(proj_ps, 1)
                if s == 31:
                    to_feat(a, ps_feat23, tok_a, xn2, NT, x2_ps)

            def logits(a):
                pe.wait_ge(x2_f, a * KT + KT)
                for t in range(NT):
                    for k in range(KT):
                        mm = pe.matmul(ps_a[0:TT, 3, t * 128:t * 128 + 128], feat_2[:, k, feat_toks[t]],
                                       gate_sb[:, k, :], start=(k == 0), stop=(k == KT - 1))
                mm.then_inc(logit_ps, 1)

            def three_passes(dst, w_cols, m, hi, lo, first, last):
                for n, (w, x) in enumerate(((w_hi, hi), (w_lo, hi), (w_hi, lo))):
                    mm = pe.matmul(dst, w[:, ATT_PIECES + m, w_cols], x, start=(first and n == 0), stop=(last and n == 2))
                return mm

            def hidden(c, m):
                if m == 0:
                    pe.wait_ge(x2_lo_ok, c * KT + KT)
                if m in (0, FIRST_LO):
                    pe.wait_ge(w_lo_ok, FIRST_LO if m == 0 else MT)
                if m >= 2:
                    pe.wait_ge(gelu_ok, c * MT + m - 1)
                for k in range(KT):
                    mm = three_passes(ps_h[:, m % 2, 0:TOK], slice(k * 128, k * 128 + 128), m,
                                      x2_hi[:, k, :], x2_lo[:, k, :], k == 0, k == KT - 1)
                mm.then_inc(hid_ps, 1)

            def back(c, m):
                pe.wait_ge(g_lo_ok, c * MT + m + 1)
                for k in range(KT):
                    mm = three_passes(ps_y[:, k, 0:TOK], slice(256 + k * 128, 256 + k * 128 + 128), m,
                                      g_hi[:, m % SBUF_G, :], g_lo[:, m % SBUF_G, :], m == 0, m == MT - 1)
                    if m == MT - 1:
                        mm.then_inc(y_done, 1)
                    elif k == KT - 1:
                        mm.then_inc(y_part, 1)

            def body(c, with_attend, with_patch):
                for m in range(MT):
                    if with_attend and m in EARLY:
                        attend(c + 1, m)
                    hidden(c, m)
                    if with_attend and m not in EARLY + LATE:
                        attend(c + 1, m)
                    if m >= LAG:
                        back(c, m - LAG)
                    if with_attend and m in LATE:
                        attend(c + 1, m)
                if with_patch:
                    patch(c + 2, 0)
                for m in range(MT - LAG, MT):
                    back(c, m)
                if with_attend:
                    logits(c + 1)
                if with_patch:
                    patch(c + 2, 1)
                if with_attend:
                    pe.wait_ge(gate_v, (c + 1) * GSTEPS + 1)
                to_tok(ps_tok23, feat_1, y_tok, y_feat, c * KT)

            def keep_clock(n, src):
                for _ in range(n):
                    pe.matmul(ps_y[:, 0, 0:256], src[:, 0:128], src[:, 0:256], start=True, stop=True)

            pe.wait_ge(blank, 1)
            keep_clock(3, feat_1[:, 0, :])
            for h, ks in enumerate(FIRST_PARTS):
                pe.wait_ge(ld_x0[h], 32)
                for mt in range(KT):
                    for k in ks:
                        mm = pe.matmul(ps_a[:, mt, 0:PTOK], lin_raw[:, k, mt * 128:mt * 128 + 128],
                                       x_raw[:, k, :], start=(k == 0), stop=(k == PKT - 1))
                    if ks.stop == PKT:
                        mm.then_inc(patch_ps, 1)
            pe.wait_ge(table, TABLES)
            pe.wait_ge(zeroed, 1)
            pe.wait_ge(ld_small, 32)
            for s in range(MT):
                if s == 6:
                    pe.wait_ge(att_pool_ok, POOL_ATT)
                    pe.wait_ge(att_lo_ok, ATT_PIECES - POOL_ATT)
                if s in KEEP_CLOCK:
                    keep_clock(KEEP_CLOCK[s], con_sb)
                attend(0, s)
                if s == 4:
                    patch_1(0)
                if s == 10:
                    patch_1(1)
            pe.wait_ge(ld_gate, 16)
            logits(0)
            pe.wait_ge(lin_lo_ok, 1)
            with pe.Fori(0, CHUNKS - 2) as c:
                body(c, True, True)
            body(CHUNKS - 2, True, False)
            body(CHUNKS - 1, False, False)

        @block.scalar
        def _(act):
            def attend(a, s, c=None):
                if s == 4:
                    act.wait_ge(x1_ps, a + 1)
                    for k in range(KT):
                        act.activation(att_hi[:, k, :], ps_feat23[:, k, :], ACT.Copy).then_inc(x1_hi, 1)
                for t in {7: (0, 1), 8: (2,)}.get(s, ()):
                    if c is not None and t == 0:
                        act.wait_ge(stored, 32 * c + 32)
                    act.wait_ge(k_relu, a * NT + t + 1)
                    act.activation(tok_b[:, t, :], tok_a[:, t, :], ACT.Square).then_inc(k_sq, 1)
                if s in (8, 10, 15):
                    t = {8: 0, 10: 1, 15: 2}[s]
                    if t == 2:
                        act.wait_ge(kvp_ps, a * NT * KT + KT)
                    for i in range(1 if t == NT - 1 else 0, TI):
                        v = act.activation(v_masked[:, t % 2, :, i * 128:i * 128 + 128],
                                           ps_a[0:TT, 1 + t, D:2 * D].rearrange("p (k e) -> p k e", k=KT),
                                           ACT.Copy, scale=img_mask[:, i:i + 1])
                    v.then_inc(v_ready, 1)
                if s == 11:
                    act.wait_ge(q_relu, a * KT + KT)
                    act.activation(feat_1[:, :, :], feat_2[:, :, :], ACT.Square).then_inc(q_sq, 1)
                if s == 22:
                    act.wait_ge(o_ps, a + 1)
                    for k in range(KT):
                        act.activation(feat_1[:, k, :], ps_a[:, 2 + k, 0:TOK], ACT.Identity,
                                       bias=b_dwc[:, k, :], scale=w_mid[:, k:k + 1]).then_inc(c_mid, 1)
                if s == 24:
                    for k in range(KT):
                        act.wait_ge(c_add, a * 2 * KT + 2 * k + 2)
                        act.activation(att_hi[:, k, :], feat_1[:, k, :], ACT.Copy).then_inc(c_hi, 1)
                if s == 31:
                    act.wait_ge(x2_ps, a + 1)
                    for k in range(KT):
                        act.activation(feat_2[:, k, :], ps_feat23[:, k, :], ACT.Copy).then_inc(x2_f, 1)

            def current(c, s):
                if s == 3:
                    act.wait_ge(h2_ready, 2 * c + 2)
                    act.activation(tok_h2c[:, :, :], tok_h2n[:, :, :], ACT.Copy).then_inc(h2_moved, 1)
                if s == 14:
                    act.wait_ge(gate_v, c * GSTEPS + 8)
                    act.activation(lg[:, 2, :, :], lg[:, 1, :, :], ACT.Tanh, scale=GATE_SCALE / 2).then_inc(gate_t, 1)

            def split_patches(c, s):
                if s == 27:
                    act.wait_ge(ld_x, 16 * c + 32)
                    act.wait_ge(proj_ps, 2 * c + 4)
                for k in SPLIT_X.get(s, ()):
                    act.activation(x_hi[:, k, :], x_raw[:, k, :], ACT.Copy).then_inc(x_hi_ok, 1)

            def body(c, with_attend, with_patch):
                for m in range(MT):
                    act.wait_ge(hid_ps, c * MT + m + 1)
                    if m >= GBUF:
                        act.wait_ge(g_lo_ok, c * MT + m - GBUF + 1)
                    act.activation(gel[:, m % GBUF, :], ps_h[:, m % 2, 0:TOK], ACT.Gelu,
                                   bias=b1_sb[:, m:m + 1]).then_inc(gelu_ok, 1)
                    current(c, m)
                    if with_attend:
                        attend(c + 1, m, c)
                    if with_patch:
                        split_patches(c, m)
                for k in range(KT):
                    act.wait_ge(y_done, c * KT + k + 1)
                    act.activation(feat_1[:, k, :], ps_y[:, k, 0:TOK], ACT.Identity,
                                   bias=b2_sum[:, k:k + 1]).then_inc(y_feat, 1)

            load_lin(act, 0)
            act.dma_start(vec_sb[:, :, :], vecs).then_inc(ld_small, 16)
            act.dma_start(con_sb[:, :], consts).then_inc(ld_small, 16)

            def split_hi(m):
                act.wait_ge(ld_w[load_of(m)], 16)
                act.activation(w_hi[:, m, :], w_raw[:, m, :], ACT.Copy).then_inc(w_hi_ok, 1)

            act.wait_ge(ld_small, 32)
            act.wait_ge(table, TABLES)
            for m in range(ATT_PIECES):
                split_hi(m)
            m = ATT_PIECES
            act.wait_ge(ld_rows, 32)
            for s in range(MT):
                attend(0, s)
                for _ in range(SPLIT_HI.get(s, 0)):
                    split_hi(m)
                    m += 1
                if s == 20:
                    act.wait_ge(patch_ps, 2 * KT)
                    act.activation(lin_hi[:, :, :], lin_raw[:, :, :], ACT.Copy).then_inc(lin_hi_ok, 1)
            with act.Fori(0, CHUNKS - 2) as c:
                body(c, True, True)
            body(CHUNKS - 2, True, False)
            body(CHUNKS - 1, False, False)

        @block.vector
        def _(dve):
            def f32(ap):
                return ap.bitcast(F32)

            def half_stats(a, src, stat):
                for t in range(NT):
                    dve.bn_stats(stats[:, t, :], src[:, t, :]).then_inc(stat, 1)

            def layer_stats(a, stat):
                base = a * LSTEPS
                dve.wait_ge(stat, base + NT)
                dve.tensor_tensor(ls[:, 0, :], stats[:, :, 1], stats[:, :, 4], ALU.add).then_inc(stat, 1)
                dve.tensor_tensor(ls[:, 1, :], stats[:, :, 1], stats[:, :, 4], ALU.subtract).then_inc(stat, 1)
                dve.tensor_tensor(ls[:, 2, :], stats[:, :, 2], stats[:, :, 5], ALU.add).then_inc(stat, 1)
                dve.wait_ge(stat, base + NT + 3)
                dve.tensor_tensor(ls[:, 3, :], ls[:, 1, :], ls[:, 1, :], ALU.mult).then_inc(stat, 1)
                dve.tensor_scalar(ls[:, 4, :], ls[:, 2, :], 1.0 / D, LN_EPS, ALU.mult, ALU.add).then_inc(stat, 1)
                dve.tensor_scalar(mean[:, :], ls[:, 0, :], 0.5, None, ALU.mult).then_inc(stat, 1)
                dve.wait_ge(stat, base + NT + 6)
                dve.scalar_tensor_tensor(out=var_e[:, :], in0=ls[:, 3, :], scalar=0.25, in1=ls[:, 4, :],
                                         op0=ALU.mult, op1=ALU.add).then_inc(stat, 1)

            def normalise(a, src, done):
                for t in range(NT):
                    dve.tensor_scalar(tok_a[:, t, :], src[:, t, :], mean[:, t:t + 1], rstd[:, t:t + 1],
                                      ALU.subtract, ALU.mult).then_inc(done, 1)

            def kv_evacuate(a, j):
                t, k = j // KT, j % KT
                dve.wait_ge(kvp_ps, a * NT * KT + j + 1)
                first = 1 if t == NT - 1 else 0
                if j == 2 * KT:
                    dve.wait_ge(num_ps, a * NT + 1)
                ps = ps_a[:, kv_bank(j), 0:KVW]
                n = TI - first
                dve.tensor_tensor(kv_sb[:, t % 2, k, first:TI, 0:128],
                                  ps[:, first * 128:TI * 128].rearrange("p (i e) -> p i e", i=n),
                                  block_mask.unsqueeze(1).to_broadcast([128, n, 128]), ALU.mult).then_inc(kvp_sb, 1)
                dve.scalar_tensor_tensor(out=kv_sb[:, t % 2, k, first:TI, 128:NUMW],
                                         in0=ps[:, TI * 128 + first:TI * 128 + TI].unsqueeze(2)
                                         .to_broadcast([128, n, HPK]),
                                         scalar=ATT_EPS,
                                         in1=head_mask.unsqueeze(1).to_broadcast([128, n, HPK]),
                                         op0=ALU.add, op1=ALU.mult).then_inc(kvp_sb, 1)

            def attend(a, s, running=False):
                heads = lambda ap: ap.rearrange("p t (h e) -> p (t h) e", e=HD)
                if s == 0:
                    dve.wait_ge(h_tok, a + 1)
                    half_stats(a, ps_tok01, stat1)
                if s == 1:
                    layer_stats(a, stat1)
                if s == 2:
                    dve.wait_ge(rstd1, a + 1)
                    normalise(a, ps_tok01, xn1)
                if s == 3:
                    dve.tensor_tensor(tok_hb[:, :, :], ps_tok01,
                                      b_proj.unsqueeze(1).to_broadcast([TT, NT, D]), ALU.add).then_inc(hb_ready, 1)
                if s == 4:
                    for k in range(KT):
                        dve.wait_ge(x1_hi, a * KT + k + 1)
                        dve.tensor_tensor(att_lo[:, k, :], ps_feat23[:, k, :], f32(att_hi[:, k, :]),
                                          ALU.subtract).then_inc(x1_lo, 1)
                for t in {7: (0, 1), 8: (2,)}.get(s, ()):
                    dve.wait_ge(kv_ps, a * NT + t + 1)
                    dve.tensor_scalar(tok_a[:, t, :], ps_a[0:TT, 1 + t, 0:D], 0.0, ATT_EPS,
                                      ALU.max, ALU.add).then_inc(k_relu, 1)
                def relu_q(k):
                    dve.wait_ge(q_ps, a * KT + k + 1)
                    dve.tensor_scalar(feat_2[:, k, :], ps_a[:, 0, 0:TOK], 0.0, ATT_EPS,
                                      ALU.max, ALU.add).then_inc(q_relu, 1)

                if s == 8:
                    relu_q(0)
                if s == 11:
                    if running:
                        dve.wait_ge(h2_moved, a)
                    dve.tensor_copy(v_masked[:, 0, :, TI * 128:KVW],
                                    img_mask.unsqueeze(1).to_broadcast([TT, KT, TI])).then_inc(masks_ok, 1)
                if s == 9:
                    dve.wait_ge(k_sq, a * NT + NT)
                    dve.tensor_tensor(tok_b[:, :, :], tok_b[:, :, :], tok_a[:, :, :], ALU.mult).then_inc(k_cube, 1)
                if s == 10:
                    dve.wait_ge(k_cube, a + 1)
                    dve.tensor_reduce(k_sum[:, :], heads(tok_b[:, :, :]), AX, ALU.add).then_inc(k_total, 1)
                    relu_q(1)
                    dve.wait_ge(k_total, a + 1)
                    dve.reciprocal(k_inv[:, :], k_sum[:, :]).then_inc(k_recip, 1)
                if s == 11:
                    dve.wait_ge(k_recip, a + 1)
                    dve.tensor_tensor(heads(tok_a[:, :, :]), heads(tok_b[:, :, :]),
                                      k_inv[:, :].unsqueeze(2).to_broadcast([TT, NT * HEADS, HD]),
                                      ALU.mult).then_inc(k_norm, 1)
                if s == 14:
                    kv_evacuate(a, 0)
                    kv_evacuate(a, 1)
                if s == 12:
                    dve.wait_ge(q_sq, a + 1)
                    for t in range(NT):
                        dve.tensor_tensor(spread(q_spread, t),
                                          feat_1[:, :, feat_toks[t]].rearrange("p k (i s) -> p k i s", i=TI),
                                          feat_2[:, :, feat_toks[t]].rearrange("p k (i s) -> p k i s", i=TI),
                                          ALU.mult).then_inc(q_cube, 1)
                if s == 15:
                    kv_evacuate(a, 2)
                if s == 16:
                    kv_evacuate(a, 3)
                    kv_evacuate(a, 4)
                    kv_evacuate(a, 5)
                if s == 20:
                    dve.wait_ge(num_ps, a * NT + NT)
                    halves = ps_a[0:TT, 1:4, :].rearrange("p t (k n) -> p (t k) n", k=KT)
                    z = z_inv[:, :].rearrange("p (g h) -> p g h", h=HPK)
                    dve.tensor_scalar(den[:, :].rearrange("p (g h) -> p g h", h=HPK), halves[:, :, 128:NUMW],
                                      TINY, None, ALU.max).then_inc(den_ok, 1)
                    dve.wait_ge(den_ok, a + 1)
                    dve.reciprocal(z_inv[:, :], den[:, :]).then_inc(z_ready, 1)
                    dve.wait_ge(z_ready, a + 1)
                    dve.tensor_tensor(tok_a[:, :, :].rearrange("p t (k h e) -> p (t k) h e", k=KT, e=HD),
                                      halves[:, :, 0:128].rearrange("p g (h e) -> p g h e", e=HD),
                                      z.unsqueeze(3).to_broadcast([TT, NT * KT, HPK, HD]), ALU.mult).then_inc(o_tok, 1)
                if s == 23:
                    o_img = ps_feat23.rearrange("p k (i s) -> p k i s", s=SEQ)
                    c_img = feat_1[:, :, :].rearrange("p k (i s) -> p k i s", s=SEQ)
                    for k in range(KT):
                        for side in range(2):
                            dst = c_img[:, k, :, 1:SEQ] if side == 0 else c_img[:, k, :, 0:SEQ - 1]
                            src = o_img[:, k, :, 0:SEQ - 1] if side == 0 else o_img[:, k, :, 1:SEQ]
                            if side == 0:
                                dve.wait_ge(c_mid, a * KT + k + 1)
                            else:
                                dve.wait_ge(c_add, a * 2 * KT + 2 * k + 1)
                            dve.scalar_tensor_tensor(out=dst, in0=src, scalar=dwc[:, k, 2 * side:2 * side + 1],
                                                     in1=dst, op0=ALU.mult, op1=ALU.add).then_inc(c_add, 1)
                if s == 24:
                    for k in range(KT):
                        dve.wait_ge(c_hi, a * KT + k + 1)
                        dve.tensor_tensor(att_lo[:, k, :], feat_1[:, k, :], f32(att_hi[:, k, :]),
                                          ALU.subtract).then_inc(c_lo, 1)
                if s == 27:
                    dve.wait_ge(hb_ready, a + 1)
                    for b, tiles in enumerate((slice(0, 2), slice(2, 3))):
                        dve.wait_ge(proj_ps, 2 * a + b + 1)
                        dve.tensor_tensor(tok_h2n[:, tiles, :], ps_tok01[:, tiles, :], tok_hb[:, tiles, :],
                                          ALU.add).then_inc(h2_ready, 1)
                    dve.wait_ge(h2_ready, 2 * a + 2)
                    half_stats(a, tok_h2n, stat2)
                if s == 28:
                    layer_stats(a, stat2)
                if s == 29:
                    dve.wait_ge(rstd2, a + 1)
                    normalise(a, tok_h2n, xn2)

            def add_gate_bias(a):
                dve.wait_ge(logit_ps, a + 1)
                logits = ps_a[0:TT, 3, 0:NT * 128].rearrange("p (t n) -> p t n", t=NT)[:, :, 0:EXPERTS]
                dve.tensor_tensor(lg[:, 0, :, :], logits,
                                  gate_b.unsqueeze(1).to_broadcast([TT, NT, EXPERTS]), ALU.add).then_inc(gate_v, 1)

            def current(a, s):
                if s == 5:
                    dve.wait_ge(gate_v, a * GSTEPS + 1)
                    dve.tensor_tensor(lg[:, 1, :, :], lg[:, 0, :, :], lg[:, 0, :, :], ALU.mult).then_inc(gate_v, 1)
                    dve.wait_ge(gate_v, a * GSTEPS + 2)
                    dve.tensor_reduce(gs[:, 0, :], lg[:, 1, :, :], AX, ALU.add).then_inc(gate_v, 1)
                    dve.wait_ge(gate_v, a * GSTEPS + 3)
                    dve.tensor_scalar(gs[:, 1, :], gs[:, 0, :], 1.0 / EXPERTS, RMS_EPS,
                                      ALU.mult, ALU.add).then_inc(gate_v, 1)
                if s == 13:
                    dve.wait_ge(gate_rms, a + 1)
                    dve.tensor_tensor(lg[:, 3, :, :], lg[:, 0, :, :],
                                      gs[:, 2, :].unsqueeze(2).to_broadcast([TT, NT, EXPERTS]),
                                      ALU.mult).then_inc(gate_v, 1)
                    dve.wait_ge(gate_v, a * GSTEPS + 5)
                    dve.tensor_tensor(lg[:, 4, :, :], lg[:, 3, :, :],
                                      rms_w.unsqueeze(1).to_broadcast([TT, NT, EXPERTS]), ALU.mult).then_inc(gate_v, 1)
                    dve.wait_ge(gate_v, a * GSTEPS + 6)
                    dve.tensor_reduce(gs[:, 3, :], lg[:, 4, :, :], AX, ALU.max).then_inc(gate_v, 1)
                    dve.wait_ge(gate_v, a * GSTEPS + 7)
                    dve.tensor_tensor(lg[:, 1, :, :], lg[:, 4, :, :],
                                      gs[:, 3, :].unsqueeze(2).to_broadcast([TT, NT, EXPERTS]),
                                      ALU.subtract).then_inc(gate_v, 1)
                if s == 17:
                    gate_end(a)

            def gate_end(a):
                dve.wait_ge(gate_t, a + 1)
                dve.tensor_scalar(lg[:, 0, :, :], lg[:, 2, :, :], 1.0, None, ALU.add).then_inc(gate_v, 1)
                dve.tensor_scalar(lg[:, 3, :, :], lg[:, 2, :, :], -1.0, 1.0, ALU.mult, ALU.add).then_inc(gate_v, 1)
                dve.wait_ge(gate_v, a * GSTEPS + 10)
                dve.reciprocal(lg[:, 4, :, :], lg[:, 3, :, :]).then_inc(gate_v, 1)
                dve.wait_ge(gate_v, a * GSTEPS + 11)
                dve.tensor_tensor(lg[:, 1, :, :], lg[:, 0, :, :], lg[:, 4, :, :], ALU.mult).then_inc(gate_v, 1)
                dve.wait_ge(gate_v, a * GSTEPS + 12)
                dve.tensor_reduce(gs[:, 4, :], lg[:, 1, :, :], AX, ALU.add).then_inc(gate_v, 1)
                dve.wait_ge(gate_v, a * GSTEPS + 13)
                dve.tensor_scalar(gs[:, 5, :], gs[:, 4, :], NORM_EPS, 1.0, ALU.mult, ALU.add).then_inc(gate_v, 1)
                dve.wait_ge(gate_v, a * GSTEPS + 14)
                dve.reciprocal(gate_n[:, :], gs[:, 5, :]).then_inc(gate_v, 1)

            def split_input(a, running):
                if running:
                    dve.wait_ge(hid_ps, a * MT)
                for k in range(KT):
                    dve.wait_ge(x2_f, a * KT + k + 1)
                    dve.tensor_copy(x2_hi[:, k, :], feat_2[:, k, :]).then_inc(x2_hi_ok, 1)
                    dve.wait_ge(x2_hi_ok, a * KT + k + 1)
                    dve.tensor_tensor(x2_lo[:, k, :], feat_2[:, k, :], f32(x2_hi[:, k, :]),
                                      ALU.subtract).then_inc(x2_lo_ok, 1)

            def add_position(p, ps=ps_a):
                for k in range(KT):
                    dve.wait_ge(patch_ps, p * KT + k + 1)
                    dve.tensor_tensor(feat_h[:, k, :, 2:SEQ],
                                      ps[:, k, 0:PTOK].rearrange("p (i s) -> p i s", i=IMG),
                                      pos_sb[:, k, :].unsqueeze(1).to_broadcast([128, IMG, PATCHES]),
                                      ALU.add).then_inc(h_feat, 1)

            def body(c, with_attend, with_patch):
                for m in range(MT):
                    if with_attend and m == 0:
                        attend(c + 1, 0, True)
                    dve.wait_ge(gelu_ok, c * MT + m + 1)
                    if m >= SBUF_G:
                        dve.wait_ge(y_part, c * (MT - 1) + m - SBUF_G + 1)
                    dve.tensor_copy(g_hi[:, m % SBUF_G, :], gel[:, m % GBUF, :]).then_inc(g_hi_ok, 1)
                    dve.wait_ge(g_hi_ok, c * MT + m + 1)
                    dve.tensor_tensor(g_lo[:, m % SBUF_G, :], gel[:, m % GBUF, :], f32(g_hi[:, m % SBUF_G, :]),
                                      ALU.subtract).then_inc(g_lo_ok, 1)
                    current(c, m)
                    if with_attend and m != 4:
                        attend(c + 1, m + 1 if m < 4 else m, True)
                if with_attend:
                    split_input(c + 1, True)
                    add_gate_bias(c + 1)
                if with_patch:
                    add_position(c + 2)
                dve.wait_ge(y_tok, c + 1)
                dve.wait_ge(h2_moved, c + 1)
                dve.wait_ge(gate_v, c * GSTEPS + GSTEPS)
                dve.wait_ge(stored, 32 * c + 32)
                for t in range(NT):
                    dve.scalar_tensor_tensor(out=tok_b[:, t, :], in0=ps_tok23[:, t, :], scalar=gate_n[:, t:t + 1],
                                             in1=tok_h2c[:, t, :], op0=ALU.mult, op1=ALU.add).then_inc(out_sb, 1)

            dve.memset(feat_1[:, 0, :], 0.0).then_inc(blank, 1)
            dve.wait_ge(ld_small, 32)
            for k in range(KT):
                dve.tensor_scalar(pos_sb[:, k, :], pos_raw[:, k, 1:SEQ - 1], blin_raw[:, k, :], None,
                                  ALU.add).then_inc(table, 1)
            for k in range(KT):
                dve.tensor_scalar(feat_h[:, k, :, 1], class_raw[:, k, :].to_broadcast([128, IMG]),
                                  pos_raw[:, k, 0:1], None, ALU.add).then_inc(table, 1)
            dve.tensor_copy(feat_h[:, 0, :, 0], cls_raw[:, 0, :].to_broadcast([128, IMG])).then_inc(table, 1)
            dve.tensor_copy(feat_h[:, 1, :, 0], cls_raw[:, 1, :].to_broadcast([128, IMG])).then_inc(table, 1)
            dve.tensor_scalar(w_mid[:, :], dwc[:, :, 1], 1.0, None, ALU.add).then_inc(table, 1)
            dve.tensor_reduce(b2_sum[:, :], b2_raw, AX, ALU.add).then_inc(table, 1)
            for k in range(KT):
                dve.tensor_copy(v_masked[:, 1, k, TI * 128:KVW], img_mask).then_inc(table, 1)
            dve.wait_ge(table, TABLES)
            dve.wait_ge(zeroed, 1)
            add_position(0)
            for s in range(MT):
                if s == 3:
                    dve.wait_ge(ld_rows, 32)
                if s in (2, 4):
                    m = POOL_ATT + s // 2 - 1
                    dve.wait_ge(w_hi_ok, m + 1)
                    dve.tensor_tensor(w_lo[:, m, :], w_raw[:, m, :], f32(w_hi[:, m, :]),
                                      ALU.subtract).then_inc(att_lo_ok, 1)
                attend(0, s)
                if s == 11:
                    add_position(1, ps_h)
                if s == 25:
                    dve.wait_ge(lin_hi_ok, 1)
                    dve.tensor_tensor(lin_lo[:, :, :], lin_raw[:, :, :], f32(lin_hi[:, :, :]),
                                      ALU.subtract).then_inc(lin_lo_ok, 1)
            split_input(0, False)
            add_gate_bias(0)
            with dve.Fori(0, CHUNKS - 2) as c:
                body(c, True, True)
            body(CHUNKS - 2, True, False)
            body(CHUNKS - 1, False, False)

        @block.gpsimd
        def _(pool):
            pool.memset(q_spread[:, :, :, :], 0.0).then_inc(zeroed_p, 1)
            pool.memset(neg_half[:, :], -0.5).then_inc(zeroed_p, 1)
            pool.wait_ge(zeroed_p, 2)
            pool.sem_inc(zeroed, 1)
            pool.sem_inc(stored, 32)

            def power(dst, src, done):
                pool.tensor_tensor(dst, src, neg_half[:, :], ALU.pow).then_inc(done, 1)

            def split_lo(pieces, done=w_lo_ok):
                for m in pieces:
                    pool.wait_ge(w_hi_ok, m + 1)
                    pool.tensor_tensor(w_lo[:, m, :], w_raw[:, m, :], w_hi[:, m, :].bitcast(F32),
                                       ALU.subtract).then_inc(done, 1)

            def norm1(a):
                pool.wait_ge(stat1, a * LSTEPS + LSTEPS)
                power(rstd[:, :], var_e[:, :], rstd1)

            def norm2(a):
                pool.wait_ge(stat2, a * LSTEPS + LSTEPS)
                power(rstd[:, :], var_e[:, :], rstd2)

            def gate(a):
                pool.wait_ge(gate_v, a * GSTEPS + 4)
                power(gs[:, 2, :], gs[:, 1, :], gate_rms)

            def patches_lo(c, pixels):
                for k in pixels:
                    pool.wait_ge(x_hi_ok, c * PKT + k + 1)
                    pool.tensor_tensor(x_lo[:, k, :], x_raw[:, k, :], x_hi[:, k, :].bitcast(F32),
                                       ALU.subtract).then_inc(x_lo_ok, 1)

            split_lo(range(0, POOL_ATT), att_pool_ok)
            norm1(0)
            split_lo(range(ATT_PIECES, ATT_PIECES + FIRST_LO))
            norm2(0)
            norm1(1)
            split_lo(range(ATT_PIECES + FIRST_LO, PIECES))
            gate(0)
            patches_lo(0, range(0, PKT // 2))
            norm2(1)
            patches_lo(0, range(PKT // 2, PKT))
            with pool.Fori(1, CHUNKS - 2) as c:
                norm1(c + 1)
                gate(c)
                patches_lo(c, range(0, PKT // 2))
                norm2(c + 1)
                patches_lo(c, range(PKT // 2, PKT))
            norm1(CHUNKS - 1)
            gate(CHUNKS - 2)
            norm2(CHUNKS - 1)
            gate(CHUNKS - 1)


def kernel(**inputs):
    import numpy as np
    import concourse.bacc as bacc
    from concourse.bass_utils import run_bass_kernel_spmd

    g = {n: np.asarray(v) for n, v in inputs.items()}

    def rows_on_partitions(w):
        return w.reshape(-1, 128, w.shape[-1]).transpose(1, 0, 2)

    x = g["x"].reshape(CHUNKS, IMG, CHAN, GRID, PATCH, GRID, PATCH).transpose(0, 2, 4, 6, 1, 3, 5)
    x = x.reshape(CHUNKS, PKT, 128, PTOK).transpose(0, 2, 1, 3)
    gate = np.zeros((D, 128), g["L0_ffn_gate_w"].dtype)
    gate[:, :EXPERTS] = g["L0_ffn_gate_w"].T
    qkv = rows_on_partitions(g["L0_attn_w_qkv"].T).reshape(128, -1, 512).transpose(1, 0, 2)
    proj = rows_on_partitions(g["L0_attn_w_proj"].T).reshape(128, -1, 512).transpose(1, 0, 2)
    w1 = g["L0_ffn_w1"].transpose(1, 0, 2).reshape(KT, 128, MT, 128).transpose(2, 1, 0, 3).reshape(MT, 128, D)
    w2 = g["L0_ffn_w2"].reshape(MT, 128, D)
    vecs = np.concatenate([g["L0_tok_position_embeddings"][0].T, g["L0_tok_class_token"][0].T, g["cls_tok"][0].T,
                           g["L0_tok_b_lin"][:, None], g["L0_attn_w_dwc"], g["L0_attn_b_dwc"][:, None],
                           g["L0_ffn_b2"].T], axis=1)
    rows = np.concatenate([g["L0_attn_b_proj"], g["L0_ffn_gate_b"], g["L0_ffn_rms_w"]])
    heads = np.arange(128) // HD
    consts = np.concatenate([np.eye(128), heads[:, None] == heads[None, :],
                             heads[:, None] == np.arange(HPK)[None, :],
                             np.arange(128)[:, None] // SEQ == np.arange(TI)[None, :]], axis=1).astype(np.float32)
    sent = {
        "x_p": x,
        "w_lin": rows_on_partitions(g["L0_tok_W_lin"].T),
        "gate_w": rows_on_partitions(gate),
        "w_pieces": np.concatenate([qkv, proj, np.concatenate([w1, w2], axis=2)]).transpose(1, 0, 2),
        "vecs": rows_on_partitions(vecs),
        "b1": g["L0_ffn_b1"].reshape(MT, 128).T,
        "rows": np.broadcast_to(rows, (TT, rows.size)),
        "consts": consts,
    }
    nc = bacc.Bacc("TRN2", target_bir_lowering=False, num_devices=1, dynamic_dma_scratch_size=1024)
    sent = {n: np.ascontiguousarray(v) for n, v in sent.items()}
    args = {n: nc.dram_tensor(n, v.shape, mybir.dt.from_np(v.dtype), kind="ExternalInput").ap() for n, v in sent.items()}
    out = nc.dram_tensor("out", (IMAGES, SEQ, D), F32, kind="ExternalOutput").ap()
    vit_block(nc, out=out.rearrange("(c i) s d -> c (i s) d", c=CHUNKS), **args)
    r = run_bass_kernel_spmd(nc, [sent], core_ids=[0])
    return r.results[0]["out"]
```
